# Optimizing a Trainium2 kernel written in Bass

```python
import numpy as np
import jax
import jax.numpy as jnp

def _softmax(x, axis=-1):
    return jax.nn.softmax(x, axis=axis)

def _gelu(x):
    return jax.nn.gelu(x, approximate=True)

def _silu(x):
    return jax.nn.silu(x)

def _sigmoid(x):
    return jax.nn.sigmoid(x)

def _layernorm(x, axis=-1, eps=1e-05):
    m = jnp.mean(x, axis=axis, keepdims=True)
    v = jnp.var(x, axis=axis, keepdims=True)
    return (x - m) / jnp.sqrt(v + eps)

def _scatter_add(tgt, idx, src, axis=0):
    return tgt.at[idx].add(src)

def _segment_sum(src, seg, n):
    return jax.ops.segment_sum(src, seg, n)
kernel_name = 'mk_flamingo_gated_d1_seqx_r8_32d50c'

def setup_inputs(seed: int=0):
    np.random.seed(seed)
    _w = jnp.asarray

    def _rec_inputs():
        import jax
        import jax.numpy as jnp
        _rk = jax.random.key(seed)
        x = -0.0002928 + 1 * jax.random.normal(jax.random.fold_in(_rk, 1), (8, 256, 128), jnp.float32)
        _lenS = 256 - jax.random.randint(jax.random.fold_in(_rk, 7), (8,), 0, max(1, 256 // 4) + 1, jnp.int32)
        _lenS2 = 256 - jax.random.randint(jax.random.fold_in(_rk, 8), (8,), 0, max(1, 256 // 4) + 1, jnp.int32)
        _ctx_1024P = jax.random.normal(jax.random.fold_in(_rk, 11), (8, 16, 128), jnp.float32)
        _ctx_1024c = jax.random.dirichlet(jax.random.fold_in(_rk, 511), 0.3 * jnp.ones((16,), jnp.float32), (8, 256))
        _ctx_1024t = jnp.einsum('bsk,bkd->bsd', _ctx_1024c, _ctx_1024P)
        _ctx_1024t = _ctx_1024t * jax.lax.rsqrt(jnp.mean(jnp.square(_ctx_1024t)) + 1e-12) * 0.953939
        ctx_1024 = -1.78809e-06 + 0.0312453 * (_ctx_1024t + 0.3 * jax.random.normal(jax.random.fold_in(_rk, 611), (8, 256, 128), jnp.float32))
        _g = jax.random.normal(jax.random.fold_in(_rk, 9001), (2, 1), jnp.float32)
        _g = jnp.sign(_g) * jnp.maximum(jnp.abs(_g), 1.0) + (_g == 0) * 1.0
        g_xattn = _g[0]
        g_ffn = _g[1]
        return (x, ctx_1024, g_xattn, g_ffn)
    x, ctx_1024, g_xattn, g_ffn = _rec_inputs()

    def _L0_xattn_setup():
        import jax, jax.numpy as jnp
        import numpy as np
        E, TPE, H, F = (64, 64, 128, 128)
        key = jax.random.key(seed)
        k1, k2, k3, k4 = jax.random.split(key, 4)
        scale = 1.0 / np.sqrt(H)
        return {'x': jax.random.normal(k1, (E, TPE, H), dtype=jnp.float32), 'w1': jax.random.normal(k2, (E, F, H), dtype=jnp.float32) * scale, 'v1': jax.random.normal(k3, (E, F, H), dtype=jnp.float32) * scale, 'w2': jax.random.normal(k4, (E, F, H), dtype=jnp.float32) * scale}
    _L0_xattn_all = _L0_xattn_setup()
    _L0_xattn_in = {k: v for k, v in _L0_xattn_all.items() if k in ()}
    del _L0_xattn_all

    def _L0_ffn_setup():
        import jax, jax.numpy as jnp
        import numpy as np
        DIM = 128
        DEPTH = 6
        HEADS = 16
        DIM_HEAD = 64
        WINDOW = 32
        INNER = HEADS * DIM_HEAD
        DIM_INNER = int(DIM * 4 * 2 / 3)
        QK_SCALE = 8.0

        def shift_tokens(t):
            a, s = jnp.split(t, 2, -1)
            s = jnp.pad(s, ((0, 0), (1, 0), (0, 0)))[:, :-1]
            return jnp.concatenate([a, s], -1)

        def l2norm(t):
            return t / jnp.maximum(jnp.linalg.norm(t, axis=-1, keepdims=True), 1e-12)

        def rotate_half(x):
            x1, x2 = jnp.split(x, 2, -1)
            return jnp.concatenate([-x2, x1], -1)

        def rotary_tables(n):
            half = jnp.arange(0, DIM_HEAD, 2, dtype=jnp.float32)
            inv_freq = 1.0 / 10000.0 ** (half / DIM_HEAD)
            t = jnp.arange(n, dtype=jnp.float32)
            freqs = t[:, None] * inv_freq[None, :]
            freqs = jnp.concatenate([freqs, freqs], -1)
            base_scale = (half + 0.4 * DIM_HEAD) / (1.4 * DIM_HEAD)
            power = (t - n // 2) / (WINDOW // 2)
            scale = base_scale[None, :] ** power[:, None]
            scale = jnp.concatenate([scale, scale], -1)
            return (freqs, scale)

        def local_attention(q, k, v):
            b, h, n, d = q.shape
            w = WINDOW
            nw = n // w
            bq = q.reshape(b, h, nw, w, d)
            bk = k.reshape(b, h, nw, w, d)
            bv = v.reshape(b, h, nw, w, d)

            def look(t):
                p = jnp.pad(t, ((0, 0), (0, 0), (1, 0), (0, 0), (0, 0)))
                return jnp.concatenate([p[:, :, :nw], p[:, :, 1:]], axis=3)
            bk2, bv2 = (look(bk), look(bv))
            seq = jnp.arange(n).reshape(nw, w)
            seq_p = jnp.pad(seq, ((1, 0), (0, 0)), constant_values=-1)
            jt = jnp.concatenate([seq_p[:nw], seq_p[1:]], axis=1)
            it = seq[:, :, None]
            jb = jt[:, None, :]
            mask = (it < jb) | (it > jb + w) | (jb == -1)
            sim = jnp.einsum('bhwie,bhwje->bhwij', bq, bk2) * QK_SCALE
            sim = jnp.where(mask, -jnp.finfo(sim.dtype).max, sim)
            attn = jax.nn.softmax(sim, -1)
            out = jnp.einsum('bhwij,bhwje->bhwie', attn, bv2)
            return out.reshape(b, h, n, d)

        def attn_layer(x, Wqkv, qs, ksc, Wo):
            b, n, _ = x.shape
            qkv = x @ Wqkv
            q, k, v = jnp.split(qkv, 3, -1)
            sh = lambda t: t.reshape(b, n, HEADS, DIM_HEAD).transpose(0, 2, 1, 3)
            q, k, v = (sh(q), sh(k), sh(v))
            q = l2norm(q) * qs
            k = l2norm(k) * ksc
            freqs, scale = rotary_tables(n)
            cos, sin = (jnp.cos(freqs), jnp.sin(freqs))
            q = q * cos * scale + rotate_half(q) * sin * scale
            inv = 1.0 / scale
            k = k * cos * inv + rotate_half(k) * sin * inv
            out = local_attention(q, k, v)
            out = out.transpose(0, 2, 1, 3).reshape(b, n, INNER)
            return out @ Wo

        def ffn_layer(x, g, bln, W1, b1, W2, b2):
            mu = x.mean(-1, keepdims=True)
            var = ((x - mu) ** 2).mean(-1, keepdims=True)
            xn = (x - mu) / jnp.sqrt(var + 1e-05) * g + bln
            hg = xn @ W1 + b1
            a, gate = jnp.split(hg, 2, -1)
            return a * jax.nn.gelu(gate, approximate=False) @ W2 + b2
        key = jax.random.key(seed)
        ks = jax.random.split(key, 8)
        B, N = (2, 256)
        init = lambda k, shape: jax.random.normal(k, shape, jnp.float32) * 0.02
        return {'x': jax.random.normal(ks[0], (B, N, DIM), jnp.float32), 'Wqkv': init(ks[1], (DEPTH, DIM, 3 * INNER)), 'q_scale': jnp.ones((DEPTH, DIM_HEAD), jnp.float32), 'k_scale': jnp.ones((DEPTH, DIM_HEAD), jnp.float32), 'Wo': init(ks[2], (DEPTH, INNER, DIM)), 'ln_g': jnp.ones((DEPTH, DIM), jnp.float32), 'ln_b': jnp.zeros((DEPTH, DIM), jnp.float32), 'W1': init(ks[3], (DEPTH, DIM, 2 * DIM_INNER)), 'b1': jnp.zeros((DEPTH, 2 * DIM_INNER), jnp.float32), 'W2': init(ks[4], (DEPTH, DIM_INNER, DIM)), 'b2': jnp.zeros((DEPTH, DIM), jnp.float32)}
    _L0_ffn_all = _L0_ffn_setup()
    _L0_ffn_in = {k: v for k, v in _L0_ffn_all.items() if k in ('Wqkv', 'q_scale', 'k_scale', 'Wo', 'ln_g', 'ln_b', 'W1', 'b1', 'W2', 'b2')}
    del _L0_ffn_all
    return {'x': x, 'ctx_1024': ctx_1024, 'g_xattn': g_xattn, 'g_ffn': g_ffn, 'L0_ffn_Wqkv': _L0_ffn_in['Wqkv'], 'L0_ffn_q_scale': _L0_ffn_in['q_scale'], 'L0_ffn_k_scale': _L0_ffn_in['k_scale'], 'L0_ffn_Wo': _L0_ffn_in['Wo'], 'L0_ffn_ln_g': _L0_ffn_in['ln_g'], 'L0_ffn_ln_b': _L0_ffn_in['ln_b'], 'L0_ffn_W1': _L0_ffn_in['W1'], 'L0_ffn_b1': _L0_ffn_in['b1'], 'L0_ffn_W2': _L0_ffn_in['W2'], 'L0_ffn_b2': _L0_ffn_in['b2']}

def reference(x, ctx_1024, g_xattn, g_ffn, L0_ffn_Wqkv, L0_ffn_q_scale, L0_ffn_k_scale, L0_ffn_Wo, L0_ffn_ln_g, L0_ffn_ln_b, L0_ffn_W1, L0_ffn_b1, L0_ffn_W2, L0_ffn_b2):
    import jax
    import jax.numpy as jnp

    def _L0_xattn_ref(x, w1, v1, w2):
        import jax, jax.numpy as jnp
        import numpy as np
        E, TPE, H, F = (64, 64, 128, 128)
        h1 = jnp.einsum('eth,efh->etf', x, w1)
        h2 = jnp.einsum('eth,efh->etf', x, v1)
        g = jax.nn.gelu(h1, approximate=False) * h2
        return jnp.einsum('etf,efh->eth', g, w2)

    def _L0_ffn_ref(x, Wqkv, q_scale, k_scale, Wo, ln_g, ln_b, W1, b1, W2, b2):
        import jax, jax.numpy as jnp
        import numpy as np
        DIM = 128
        DEPTH = 6
        HEADS = 16
        DIM_HEAD = 64
        WINDOW = 32
        INNER = HEADS * DIM_HEAD
        DIM_INNER = int(DIM * 4 * 2 / 3)
        QK_SCALE = 8.0

        def shift_tokens(t):
            a, s = jnp.split(t, 2, -1)
            s = jnp.pad(s, ((0, 0), (1, 0), (0, 0)))[:, :-1]
            return jnp.concatenate([a, s], -1)

        def l2norm(t):
            return t / jnp.maximum(jnp.linalg.norm(t, axis=-1, keepdims=True), 1e-12)

        def rotate_half(x):
            x1, x2 = jnp.split(x, 2, -1)
            return jnp.concatenate([-x2, x1], -1)

        def rotary_tables(n):
            half = jnp.arange(0, DIM_HEAD, 2, dtype=jnp.float32)
            inv_freq = 1.0 / 10000.0 ** (half / DIM_HEAD)
            t = jnp.arange(n, dtype=jnp.float32)
            freqs = t[:, None] * inv_freq[None, :]
            freqs = jnp.concatenate([freqs, freqs], -1)
            base_scale = (half + 0.4 * DIM_HEAD) / (1.4 * DIM_HEAD)
            power = (t - n // 2) / (WINDOW // 2)
            scale = base_scale[None, :] ** power[:, None]
            scale = jnp.concatenate([scale, scale], -1)
            return (freqs, scale)

        def local_attention(q, k, v):
            b, h, n, d = q.shape
            w = WINDOW
            nw = n // w
            bq = q.reshape(b, h, nw, w, d)
            bk = k.reshape(b, h, nw, w, d)
            bv = v.reshape(b, h, nw, w, d)

            def look(t):
                p = jnp.pad(t, ((0, 0), (0, 0), (1, 0), (0, 0), (0, 0)))
                return jnp.concatenate([p[:, :, :nw], p[:, :, 1:]], axis=3)
            bk2, bv2 = (look(bk), look(bv))
            seq = jnp.arange(n).reshape(nw, w)
            seq_p = jnp.pad(seq, ((1, 0), (0, 0)), constant_values=-1)
            jt = jnp.concatenate([seq_p[:nw], seq_p[1:]], axis=1)
            it = seq[:, :, None]
            jb = jt[:, None, :]
            mask = (it < jb) | (it > jb + w) | (jb == -1)
            sim = jnp.einsum('bhwie,bhwje->bhwij', bq, bk2) * QK_SCALE
            sim = jnp.where(mask, -jnp.finfo(sim.dtype).max, sim)
            attn = jax.nn.softmax(sim, -1)
            out = jnp.einsum('bhwij,bhwje->bhwie', attn, bv2)
            return out.reshape(b, h, n, d)

        def attn_layer(x, Wqkv, qs, ksc, Wo):
            b, n, _ = x.shape
            qkv = x @ Wqkv
            q, k, v = jnp.split(qkv, 3, -1)
            sh = lambda t: t.reshape(b, n, HEADS, DIM_HEAD).transpose(0, 2, 1, 3)
            q, k, v = (sh(q), sh(k), sh(v))
            q = l2norm(q) * qs
            k = l2norm(k) * ksc
            freqs, scale = rotary_tables(n)
            cos, sin = (jnp.cos(freqs), jnp.sin(freqs))
            q = q * cos * scale + rotate_half(q) * sin * scale
            inv = 1.0 / scale
            k = k * cos * inv + rotate_half(k) * sin * inv
            out = local_attention(q, k, v)
            out = out.transpose(0, 2, 1, 3).reshape(b, n, INNER)
            return out @ Wo

        def ffn_layer(x, g, bln, W1, b1, W2, b2):
            mu = x.mean(-1, keepdims=True)
            var = ((x - mu) ** 2).mean(-1, keepdims=True)
            xn = (x - mu) / jnp.sqrt(var + 1e-05) * g + bln
            hg = xn @ W1 + b1
            a, gate = jnp.split(hg, 2, -1)
            return a * jax.nn.gelu(gate, approximate=False) @ W2 + b2
        for i in range(DEPTH):
            x = attn_layer(shift_tokens(x), Wqkv[i], q_scale[i], k_scale[i], Wo[i]) + x
            x = ffn_layer(shift_tokens(x), ln_g[i], ln_b[i], W1[i], b1[i], W2[i], b2[i]) + x
        return x
    x = x + jnp.tanh(g_xattn[0]) * _L0_xattn_ref(_layernorm(x, axis=-1), ctx_1024, ctx_1024, ctx_1024)
    x = x + jnp.tanh(g_ffn[0]) * _L0_ffn_ref(_layernorm(x, axis=-1), L0_ffn_Wqkv, L0_ffn_q_scale, L0_ffn_k_scale, L0_ffn_Wo, L0_ffn_ln_g, L0_ffn_ln_b, L0_ffn_W1, L0_ffn_b1, L0_ffn_W2, L0_ffn_b2)
    return x

_drawn_inputs = setup_inputs


def setup_inputs(seed=0):
    import zlib

    import numpy as np

    out = dict(_drawn_inputs(seed))
    spreads = {'L0_ffn_q_scale': (1.0, 0.2),
     'L0_ffn_k_scale': (1.0, 0.2),
     'L0_ffn_ln_g': (1.0, 0.6),
     'L0_ffn_ln_b': (0.0, 0.702),
     'L0_ffn_b1': (0.0, 0.1),
     'L0_ffn_b2': (0.0, 0.1)}
    factors = {}
    for name, (base, spread) in spreads.items():
        noise = np.random.default_rng([zlib.crc32(name.encode()), seed]).standard_normal(out[name].shape)
        drawn = base * np.exp(spread * noise) if base else spread * noise
        out[name] = jnp.asarray(drawn.astype(out[name].dtype))
    for name, factor in factors.items():
        out[name] = (out[name] * factor).astype(out[name].dtype)
    return out
```

```python
from contextlib import ExitStack

import concourse.bass as bass
from concourse import mybir

F32 = mybir.dt.float32
ALU = mybir.AluOpType
ACT = mybir.ActivationFunctionType
AX_X = mybir.AxisListType.X

P = 128
NB = 8
SEQ = 256
TILES = SEQ // P
D = 128
DEPTH = 6
HEADS = 16
DH = 64
HALF = DH // 2
WIN = 32
NWT = P // WIN
INNER = HEADS * DH
BLK = INNER // P
FF = int(D * 4 * 2 / 3)
FC = [(0, 128), (128, 128), (256, FF - 256)]
CH = 512
HPC = CH // DH
NBL = NB * DEPTH
EPS = 1e-5
QK_SCALE = 8.0
BANDW = P + WIN


def flamingo_kernel(nc, x, ctx, g_xattn, g_ffn, wqkv, q_scale, k_scale, wo, ln_g, ln_b, w1, b1, w2, b2,
                    c_cos, c_sin, c_mask, c_ident, c_shift, c_carry, out):
    x_v = x.rearrange("b (t p) d -> p (b t) d", p=P)
    ctx_v = ctx.rearrange("b (t p) d -> p (b t) d", p=P)
    out_v = out.rearrange("b (t p) d -> p (b t) d", p=P)

    with ExitStack() as es:
        def sb(name, shape):
            return es.enter_context(nc.sbuf_tensor(name, shape, F32))

        def bank(name, shape):
            return es.enter_context(nc.psum_tensor(name, shape, F32))

        def sem(name):
            return es.enter_context(nc.semaphore(name))

        Wqkv = sb("Wqkv", [P, 2, 3 * INNER])
        Wo = sb("Wo", [P, 2, BLK, D])
        W1 = sb("W1", [P, DEPTH, 2 * FF])
        W1c = sb("W1c", [P, 2 * FF])
        W2 = sb("W2", [P, DEPTH, len(FC), D])
        B1 = sb("B1", [P, DEPTH, 2, len(FC)])
        B2 = sb("B2", [P, DEPTH, D])
        G = sb("G", [P, DEPTH])
        Bt = sb("Bt", [P, DEPTH])
        TA = sb("TA", [P, DEPTH, TILES * 2 * DH])
        TB = sb("TB", [P, DEPTH, TILES * 2 * DH])
        cosc = sb("cosc", [P, TILES * 2 * DH])
        sinc = sb("sinc", [P, TILES * 2 * DH])
        mask = sb("mask", [P, TILES, 2 * WIN])
        ident = sb("ident", [P, P])
        shift = sb("shift", [P, P])
        carry = sb("carry", [P, P])
        negh = sb("negh", [P, HEADS])
        gates = sb("gates", [P, 2])
        tg = sb("tg", [P, 2])
        X1 = sb("X1", [P, NB * TILES, D])
        Y = sb("Y", [P, NB * TILES, D])
        YA = sb("YA", [P, TILES, D])
        YT = sb("YT", [P, SEQ])
        SQ = sb("SQ", [P, 2, CH])
        SSQ = sb("SSQ", [P, TILES, 2, HEADS])
        RN = sb("RN", [P, 2, HEADS])
        T1 = sb("T1", [P, TILES, 2, INNER])
        T2 = sb("T2", [P, 2, INNER])
        QT = sb("QT", [P, BLK, SEQ])
        KT = sb("KT", [P, BLK, WIN + SEQ])
        V = sb("V", [P, 2, TILES, INNER])
        PB = sb("PB", [P, TILES, HEADS, 2 * WIN])
        MX = sb("MX", [P, HEADS])
        SS = sb("SS", [P, HEADS])
        RS = sb("RS", [P, TILES, HEADS])
        BAND = [sb("BAND0", [P, HEADS, BANDW]), sb("BAND1", [P, HEADS, P])]
        OTS = sb("OTS", [P, BLK, SEQ])
        YC = sb("YC", [P, TILES, D])
        YCB = sb("YCB", [P, TILES, D])
        XS = sb("XS", [P, TILES, D])
        XN = sb("XN", [P, TILES, D])
        XNT = sb("XNT", [P, SEQ])
        BS = sb("BS", [P, TILES, 6])
        MV = sb("MV", [P, TILES, 2])
        RV = sb("RV", [P, TILES])
        G1 = sb("G1", [P, 2 * SEQ])
        U = sb("U", [P, len(FC), SEQ])
        CTX = T2[:, :, :].rearrange("p a n -> p (a n)").rearrange("p (k d) -> p k d", d=D)
        CTS = YC
        CTT = QT[:, 0, :]
        QS = QT[:, 1:4, :].rearrange("p a n -> p (a n)").rearrange("p (l n) -> p l n", l=DEPTH)

        KB = [bank(f"KB{i}", [P, CH]) for i in range(2)]
        TQ = [bank(f"TQ{i}", [P, CH]) for i in range(2)]
        SP = [bank(f"SP{i}", [P, BLK, 2 * WIN]) for i in range(2)]
        M0 = bank("M0", [P, CH])
        M1 = bank("M1", [P, CH])
        M0t = M0[:, 0:TILES * D].rearrange("p (t d) -> p t d", t=TILES)

        x_in = sem("x_in")
        ctx_in = sem("ctx_in")
        const_in = sem("const_in")
        scale_in = sem("scale_in")
        small_in = sem("small_in")
        ffn_in = sem("ffn_in")
        wqkv_in = sem("wqkv_in")
        wo_in = sem("wo_in")
        zeroed = sem("zeroed")
        tanh_done = sem("tanh_done")
        tab_done = sem("tab_done")
        f_bn = sem("f_bn")
        f_mv = sem("f_mv")
        f_eps = sem("f_eps")
        f_rv = sem("f_rv")
        f_xn = sem("f_xn")
        f_cts = sem("f_cts")
        f_tr = sem("f_tr")
        f_ev = sem("f_ev")
        f_h = sem("f_h")
        f_gelu = sem("f_gelu")
        f_u = sem("f_u")
        f_o = sem("f_o")
        f_x1 = sem("f_x1")
        ya_copied = sem("ya_copied")
        xt_mm = sem("xt_mm")
        yt_ready = sem("yt_ready")
        chunk_mm = sem("chunk_mm")
        v_evac = sem("v_evac")
        sq_done = sem("sq_done")
        rope_done = sem("rope_done")
        sq_summed = sem("sq_summed")
        t2_used = sem("t2_used")
        ss_clamped = sem("ss_clamped")
        rnorm = sem("rnorm")
        t1_ready = sem("t1_ready")
        fill_mm = sem("fill_mm")
        fill_evac = sem("fill_evac")
        sims_mm = sem("sims_mm")
        s_masked = sem("s_masked")
        s_max = sem("s_max")
        s_shifted = sem("s_shifted")
        p_exp = sem("p_exp")
        p_sum = sem("p_sum")
        p_rsum = sem("p_rsum")
        p_ready = sem("p_ready")
        band_ready = sem("band_ready")
        pj_mm = sem("pj_mm")
        yc_ready = sem("yc_ready")
        fx_mm = sem("fx_mm")
        xs_hi = sem("xs_hi")
        xs_lo = sem("xs_lo")
        ycb_ready = sem("ycb_ready")
        bn_done = sem("bn_done")
        mv_done = sem("mv_done")
        var_eps = sem("var_eps")
        rv_done = sem("rv_done")
        xn_ready = sem("xn_ready")
        ft_mm = sem("ft_mm")
        xnt_ready = sem("xnt_ready")
        w1c_ready = sem("w1c_ready")
        h_mm = sem("h_mm")
        g_ready = sem("g_ready")
        u_done = sem("u_done")
        po_mm = sem("po_mm")
        y_ready = sem("y_ready")
        o_ready = sem("o_ready")
        out_done = sem("out_done")
        waited = sem("waited")

        def wide(ap, dim, n):
            shape = list(ap.shape)
            shape[dim] = n
            return ap.broadcast_to(shape)

        def batch(n):
            return bass.ds((n & (NB - 1)) * TILES, TILES)

        def layer(n):
            if isinstance(n, int):
                return n // NB
            return nc.s_assert_within(n // NB, 0, DEPTH - 1,
                                      skip_runtime_bounds_check_because="steps end before NBL = NB * DEPTH")

        def one(i):
            return bass.ds(i, 1)

        def after(eng, s, count):
            if not isinstance(count, int) or count > 0:
                eng.wait_ge(s, count)

        def apart(eng):
            eng.sem_inc(waited, 1)

        def pipeline(eng, step):
            step(0, 0, True, False, False)
            step(1, 1, True, True, False)
            with eng.Fori(2, NBL, 2) as i:
                step(i, 0, True, True, True)
                step(i + 1, 1, True, True, True)
            step(NBL, 0, False, True, True)
            step(NBL + 1, 1, False, False, True)

        block = es.enter_context(nc.Block())

        @block.sync
        def _(sp):
            sp.dma_start(X1[:, :, :], x_v).then_inc(x_in, 16)
            sp.dma_start(CTX, ctx_v).then_inc(ctx_in, 16)
            sp.dma_start(ident[:, :], c_ident).then_inc(const_in, 16)
            sp.dma_start(shift[:, :], c_shift).then_inc(const_in, 16)
            sp.dma_start(carry[:, :], c_carry).then_inc(const_in, 16)
            sp.dma_start(cosc[:, :], c_cos).then_inc(const_in, 16)
            sp.dma_start(sinc[:, :], c_sin).then_inc(const_in, 16)
            sp.dma_start(mask[:, :, :].rearrange("p t n -> p (t n)"), c_mask).then_inc(const_in, 16)
            sp.dma_start(gates[:, 0:1], wide(g_xattn.rearrange("(a n) -> a n", a=1), 0, P)).then_inc(const_in, 16)
            sp.dma_start(gates[:, 1:2], wide(g_ffn.rearrange("(a n) -> a n", a=1), 0, P)).then_inc(const_in, 16)
            for l in range(DEPTH):
                sp.dma_start(QS[:, l, 0:DH], wide(q_scale[l:l + 1, :], 0, P)).then_inc(scale_in, 16)
                sp.dma_start(QS[:, l, DH:2 * DH], wide(k_scale[l:l + 1, :], 0, P)).then_inc(scale_in, 16)
            sp.dma_start(W1[:, :, :], w1.rearrange("l d n -> d l n")).then_inc(ffn_in, 16)
            for c, (f0, fn) in enumerate(FC):
                sp.dma_start(W2[0:fn, :, c, :], w2[:, f0:f0 + fn, :].rearrange("l f d -> f l d")).then_inc(ffn_in, 16)
            sp.dma_start(B2[:, :, :], wide(b2.rearrange("(a l) d -> a l d", a=1), 0, P)).then_inc(small_in, 16)
            sp.dma_start(G[:, :], ln_g).then_inc(small_in, 16)
            sp.dma_start(Bt[:, :], ln_b).then_inc(small_in, 16)
            sp.dma_start(B1[:, :, :, :].rearrange("p l h c -> p (l h c)"), b1).then_inc(small_in, 16)

            def load_layer(l, slot):
                sp.dma_start(Wqkv[:, one(slot), :].rearrange("p a n -> p (a n)"),
                             wqkv[one(l), :, :].rearrange("a d n -> (a d) n")).then_inc(wqkv_in, 16)
                sp.dma_start(Wo[:, one(slot), :, :].rearrange("p a k d -> p (a k) d"),
                             wo[one(l), :, :].rearrange("a (k p) d -> p (a k) d", p=P)).then_inc(wo_in, 16)

            load_layer(0, 0)
            sp.wait_ge(wqkv_in, 16)
            sp.wait_ge(wo_in, 16)
            load_layer(1, 1)
            with sp.Fori(2, DEPTH, 1) as l:
                sp.wait_ge(wqkv_in, 16 * l)
                sp.wait_ge(wo_in, 16 * l)
                sp.wait_ge(pj_mm, (l - 1) * NB)
                apart(sp)
                load_layer(l, l & 1)
            sp.wait_ge(o_ready, 1)
            sp.dma_start(out_v, Y[:, :, :]).then_inc(out_done, 16)
            sp.wait_ge(out_done, 16)

        @block.tensor
        def _(pe):
            mm, tr = pe.matmul, pe.transpose

            pe.wait_ge(const_in, 16 * 8)
            with pe.Fori(0, NB, 1) as b:
                pe.wait_ge(f_xn, b + 1)
                pe.wait_ge(f_cts, b + 1)
                for t in range(TILES):
                    tr(M0[:, t * P:(t + 1) * P], XN[:, t, :], ident[:, :])
                for t in range(TILES):
                    last = tr(TQ[0][:, t * P:(t + 1) * P], CTS[:, t, :], ident[:, :])
                last.then_inc(f_tr, 1)
                pe.wait_ge(f_ev, b + 1)
                for f in range(TILES):
                    last = mm(M1[:, f * SEQ:(f + 1) * SEQ], CTT[:, f * P:(f + 1) * P], XNT[:, :],
                              start=True, stop=True)
                last.then_inc(f_h, 1)
                pe.wait_ge(f_u, b + 1)
                for t in range(TILES):
                    for f in range(TILES):
                        last = mm(KB[0][:, t * D:(t + 1) * D], U[:, f, t * P:(t + 1) * P], CTS[:, f, :],
                                  start=(f == 0), stop=(f == TILES - 1))
                last.then_inc(f_o, 1)
            pe.wait_ge(f_x1, NB)

            def step(n, odd, a, b, d):
                m, q = n - 1, n - 2
                if a:
                    pe.wait_ge(ya_copied, n + 1)
                    after(pe, yc_ready, n - 1)
                    for t in range(TILES):
                        last = tr(M0[:, t * P:(t + 1) * P], YA[:, t, :], ident[:, :])
                    last.then_inc(xt_mm, 1)
                if b:
                    sims(m, 0)
                if d:
                    if a:
                        pe.wait_ge(yt_ready, n + 1)
                    pe.wait_ge(yc_ready, q + 1)
                    fx = M0[:, 0:TILES * HALF * 2].rearrange("p (t d) -> p t d", t=TILES)
                    mm(fx, shift[:, :], YC[:, :, D // 2:D], start=True, stop=False, skip_group_check=True)
                    mm(fx[:, 1, :], carry[:, :], YC[:, 0, D // 2:D], start=False, stop=True,
                       skip_group_check=True).then_inc(fx_mm, 1)
                if a:
                    qkv(n, 0)
                if b:
                    sims(m, 1)
                if d:
                    pe.wait_ge(xn_ready, q + 1)
                    for t in range(TILES):
                        last = tr(M0[:, t * P:(t + 1) * P], XN[:, t, :], ident[:, :])
                    last.then_inc(ft_mm, 1)
                if a:
                    qkv(n, 1)
                if d:
                    ffn(q)
                if b:
                    attend(m, 1 - odd, n if a else None)
                if a:
                    turn(n)

            def qkv(n, t):
                pe.wait_ge(yt_ready, n + 1)
                pe.wait_ge(wqkv_in, 16 * (layer(n) + 1))
                for j, c in enumerate((4, 5, 0, 1, 2, 3)):
                    if j < 2:
                        after(pe, rope_done, 8 * n + 4 * t - 1 + j)
                    elif j < 4:
                        pe.wait_ge(v_evac, 4 * n + 2 * t + j - 1)
                    else:
                        pe.wait_ge(rope_done, 8 * n + 4 * t + j - 3)
                    mm(KB[j % 2][:, :], YT[:, t * P:(t + 1) * P],
                       Wqkv[:, one(layer(n) & 1), c * CH:(c + 1) * CH].rearrange("p a n -> p (a n)"),
                       start=True, stop=True).then_inc(chunk_mm, 1)

            def turn(n):
                for t in range(TILES):
                    for g in range(4):
                        if g % 2 == 0:
                            pe.wait_ge(t1_ready, 4 * n + 2 * t + g // 2 + 1)
                        f = 12 * n + 4 * t + g
                        after(pe, fill_evac, f - 1)
                        for k in range(4):
                            c = (g % 2) * CH + k * P
                            last = tr(TQ[g % 2][:, k * P:(k + 1) * P], T1[:, t, g // 2, c:c + P], ident[:, :])
                        last.then_inc(fill_mm, 1)

            def sims(m, t):
                pe.wait_ge(fill_evac, 12 * m + 8)
                after(pe, s_masked, 2 * m + t)
                apart(pe)
                for blk in range(BLK):
                    for w in range(NWT):
                        for a in range(2):
                            rows = slice(DH * a, DH * a + DH)
                            c = t * P + w * WIN
                            last = mm(SP[a][WIN * w:WIN * w + WIN, blk, :], QT[rows, blk, c:c + WIN],
                                      KT[rows, blk, c:c + 2 * WIN], start=True, stop=True)
                last.then_inc(sims_mm, 1)

            def attend(m, odd, n):
                pe.wait_ge(band_ready, m + 1)
                pe.wait_ge(v_evac, 4 * m + 4)
                vp = V[:, odd, :, :]
                for k in range(4):
                    after(pe, fill_evac, 12 * m + 8 + k - 1)
                    for i in range(2):
                        blk = 2 * k + i
                        for a in range(2):
                            h = 2 * blk + a
                            o = TQ[k % 2][DH * a:DH * a + DH, i * SEQ:(i + 1) * SEQ]
                            mm(o[:, P:SEQ], vp[:, 1, h * DH:(h + 1) * DH], BAND[1][:, a * BLK + blk, :],
                               start=True, stop=False, skip_group_check=True)
                            last = mm(o[:, 0:BANDW], vp[:, 0, h * DH:(h + 1) * DH], BAND[0][:, a * BLK + blk, :],
                                      start=False, stop=True, skip_group_check=True)
                    last.then_inc(fill_mm, 1)
                pe.wait_ge(fill_evac, 12 * m + 12)
                pe.wait_ge(y_ready, NB + m)
                if n is not None:
                    pe.wait_ge(yt_ready, n + 1)
                pe.wait_ge(wo_in, 16 * (layer(m) + 1))
                for t in range(TILES):
                    for blk in range(BLK):
                        last = mm(M0t[:, t, :], OTS[:, blk, t * P:(t + 1) * P],
                                  Wo[:, one(layer(m) & 1), blk, :].rearrange("p a d -> p (a d)"),
                                  start=(blk == 0), stop=(blk == BLK - 1))
                last.then_inc(pj_mm, 1)

            def ffn(q):
                pe.wait_ge(xnt_ready, q + 1)
                pe.wait_ge(w1c_ready, q + 1)
                for c, (f0, fn) in enumerate(FC):
                    after(pe, u_done, 3 * q + c)
                    for half in range(2):
                        last = mm(M1[0:fn, half * SEQ:(half + 1) * SEQ],
                                  W1c[:, half * FF + f0:half * FF + f0 + fn], XNT[:, :], start=True, stop=True)
                    last.then_inc(h_mm, 1)
                pe.wait_ge(u_done, 3 * q + 3)
                for t in range(TILES):
                    for c, (f0, fn) in enumerate(FC):
                        last = mm(M0t[:, t, :], U[0:fn, c, t * P:(t + 1) * P],
                                  W2[0:fn, one(layer(q)), c, :].rearrange("p a d -> p (a d)"),
                                  start=(c == 0), stop=(c == len(FC) - 1))
                last.then_inc(po_mm, 1)

            pipeline(pe, step)

        @block.scalar
        def _(act):
            f = act.activation
            act.wait_ge(const_in, 16 * 8)
            f(tg[:, :], gates[:, :], ACT.Tanh).then_inc(tanh_done, 1)
            act.wait_ge(ctx_in, 16)
            with act.Fori(0, NB, 1) as b:
                after(act, f_o, b) if isinstance(b, int) else None
                f(CTS[:, :, :], CTX[:, batch(b), :], ACT.Copy).then_inc(f_cts, 1)
                act.wait_ge(f_tr, b + 1)
                f(XNT[:, :], M0[:, 0:SEQ], ACT.Copy)
                f(CTT, TQ[0][:, 0:SEQ], ACT.Copy).then_inc(f_ev, 1)
                act.wait_ge(f_h, b + 1)
                f(G1[:, :], M1[:, :], ACT.Gelu).then_inc(f_gelu, 1)
                act.wait_ge(f_o, b + 1)

            def step(n, odd, a, b, d):
                m, q = n - 1, n - 2
                if a:
                    pe_free = n
                    act.wait_ge(y_ready, n + 1)
                    after(act, xt_mm, pe_free)
                    f(YA[:, :, :], Y[:, batch(n), :], ACT.Copy).then_inc(ya_copied, 1)
                    act.wait_ge(xt_mm, n + 1)
                    f(YT[0:D // 2, :], M0[0:D // 2, 0:SEQ], ACT.Copy)
                    f(YT[D // 2:D, 1:SEQ], M0[D // 2:D, 0:SEQ - 1], ACT.Copy).then_inc(yt_ready, 1)
                if d:
                    act.wait_ge(fx_mm, q + 1)
                    f(XS[:, :, D // 2:D], M0[:, 0:TILES * D // 2].rearrange("p (t d) -> p t d", t=TILES),
                      ACT.Copy).then_inc(xs_hi, 1)
                    after(act, h_mm, 3 * q)
                    act.wait_ge(ffn_in, 16 * 4)
                    f(W1c[:, :], W1[:, one(layer(q)), :].rearrange("p a n -> p (a n)"), ACT.Copy).then_inc(w1c_ready, 1)
                if b:
                    exps(m, 0)
                if a:
                    evac_qkv(n, 0, odd)
                if d:
                    act.wait_ge(ft_mm, q + 1)
                    act.wait_ge(small_in, 16 * 4)
                    f(XNT[:, :], M0[:, 0:SEQ], ACT.Identity, bias=Bt[:, one(layer(q))],
                      scale=G[:, one(layer(q))]).then_inc(xnt_ready, 1)
                if b:
                    exps(m, 1)
                if a:
                    evac_qkv(n, 1, odd)
                if d:
                    for c, (f0, fn) in enumerate(FC):
                        act.wait_ge(h_mm, 3 * q + c + 1)
                        f(G1[0:fn, 0:SEQ], M1[0:fn, SEQ:2 * SEQ], ACT.Gelu,
                          bias=B1[0:fn, one(layer(q)), 1, c]).then_inc(g_ready, 1)
                if b:
                    for k in range(4):
                        act.wait_ge(fill_mm, 12 * m + 8 + k + 1)
                        f(OTS[:, 2 * k:2 * k + 2, :], TQ[k % 2][:, :].rearrange("p (k n) -> p k n", k=2),
                          ACT.Copy).then_inc(fill_evac, 1)
                if a:
                    for t in range(TILES):
                        for g in range(4):
                            act.wait_ge(fill_mm, 12 * n + 4 * t + g + 1)
                            to, c0 = (QT, t * P) if g < 2 else (KT, WIN + t * P)
                            f(to[:, 4 * (g % 2):4 * (g % 2) + 4, c0:c0 + P],
                              TQ[g % 2][:, :].rearrange("p (k n) -> p k n", k=4), ACT.Copy).then_inc(fill_evac, 1)

            def exps(m, t):
                act.wait_ge(s_shifted, 2 * m + t + 1)
                f(PB[:, t, :, :], PB[:, t, :, :], ACT.Exp, scale=QK_SCALE).then_inc(p_exp, 1)

            def evac_qkv(n, t, odd):
                for j in range(2):
                    act.wait_ge(chunk_mm, 12 * n + 6 * t + j + 1)
                    f(V[:, odd, t, j * CH:(j + 1) * CH], KB[j][:, :], ACT.Copy).then_inc(v_evac, 1)
                for c in range(4):
                    act.wait_ge(chunk_mm, 12 * n + 6 * t + 2 + c + 1)
                    after(act, sq_summed, 8 * n + 4 * t + c - 1)
                    f(SQ[:, c % 2, :], KB[c % 2][:, :], ACT.Square).then_inc(sq_done, 1)

            pipeline(act, step)

        @block.vector
        def _(dve):
            tt, ts, stt = dve.tensor_tensor, dve.tensor_scalar, dve.scalar_tensor_tensor
            dve.memset(YT[D // 2:D, 0:1], 0.0).then_inc(zeroed, 1)
            dve.memset(KT[:, :, 0:WIN], 0.0).then_inc(zeroed, 1)

            def stats(src, k, bn, mv):
                apart(dve)
                for t in range(TILES):
                    last = dve.bn_stats(BS[:, t, :], src(t))
                last.then_inc(bn, 1)
                dve.wait_ge(bn, k + 1)
                apart(dve)
                for t in range(TILES):
                    last = dve.bn_aggr(MV[:, t, :], BS[:, t, :])
                last.then_inc(mv, 1)

            dve.wait_ge(x_in, 16)
            dve.wait_ge(tanh_done, 1)
            with dve.Fori(0, NB, 1) as b:
                def x_tile(t):
                    return X1[:, one(b * TILES + t), :].rearrange("p a d -> p (a d)")

                stats(x_tile, 2 * b, f_bn, f_mv)
                dve.wait_ge(f_rv, 2 * b + 1)
                for t in range(TILES):
                    last = ts(XN[:, t, :], x_tile(t), MV[:, t, 0:1], RV[:, t:t + 1], ALU.subtract, ALU.mult)
                last.then_inc(f_xn, 1)
                dve.wait_ge(f_gelu, b + 1)
                tt(U[:, 0:2, :].rearrange("p f n -> p (f n)"), M1[:, :], G1[:, :], ALU.mult).then_inc(f_u, 1)
                dve.wait_ge(f_o, b + 1)
                stt(out=X1[:, batch(b), :], in0=KB[0][:, 0:TILES * D].rearrange("p (t d) -> p t d", t=TILES),
                    scalar=tg[:, 0:1], in1=X1[:, batch(b), :], op0=ALU.mult, op1=ALU.add).then_inc(f_x1, 1)
                dve.wait_ge(f_x1, b + 1)
                stats(x_tile, 2 * b + 1, f_bn, f_mv)
                dve.wait_ge(f_rv, 2 * b + 2)
                for t in range(TILES):
                    last = ts(Y[:, one(b * TILES + t), :].rearrange("p a d -> p (a d)"), x_tile(t),
                              MV[:, t, 0:1], RV[:, t:t + 1], ALU.subtract, ALU.mult)
                last.then_inc(y_ready, 1)

            dve.wait_ge(scale_in, 16 * 2 * DEPTH)
            dve.wait_ge(const_in, 16 * 8)
            qs = QS[:, :, :].rearrange("p l (c s d) -> p l c s d", c=2, s=2)
            for l in range(DEPTH):
                for t in range(TILES):
                    cols = slice(t * 2 * DH, (t + 1) * 2 * DH)
                    tt(TA[:, l, cols], cosc[:, cols], QS[:, l, :], ALU.mult)
                    last = tt(TB[:, l, cols].rearrange("p (c s d) -> p c s d", c=2, s=2),
                              sinc[:, cols].rearrange("p (c s d) -> p c s d", c=2, s=2),
                              qs[:, l, :, ::-1, :], ALU.mult)
            last.then_inc(tab_done, 1)
            dve.wait_ge(tab_done, 1)

            def step(n, odd, a, b, d):
                m, q = n - 1, n - 2
                if b:
                    scores(m, 0)
                if d:
                    dve.wait_ge(xs_hi, q + 1)
                    dve.wait_ge(xs_lo, q + 1)
                    stats(lambda t: XS[:, t, :], q, bn_done, mv_done)
                if a:
                    rope(n, 0)
                if b:
                    sums(m, 0)
                if d:
                    dve.wait_ge(rv_done, q + 1)
                    for t in range(TILES):
                        last = ts(XN[:, t, :], XS[:, t, :], MV[:, t, 0:1], RV[:, t:t + 1], ALU.subtract, ALU.mult)
                    last.then_inc(xn_ready, 1)
                if b:
                    scores(m, 1)
                    dve.wait_ge(p_ready, 2 * m + 1)
                    after(dve, fill_mm, 12 * m)
                    dve.wait_ge(zeroed, 4)
                    for v in range(NWT):
                        band(0, v, 0, v, WIN, v * WIN)
                        if v < NWT - 1:
                            band(0, v, 0, v + 1, 0, (v + 1) * WIN)
                if a:
                    rope(n, 1)
                if b:
                    sums(m, 1)
                if d:
                    for c, (f0, fn) in enumerate(FC):
                        dve.wait_ge(g_ready, 3 * q + c + 1)
                        stt(out=U[0:fn, c, :], in0=M1[0:fn, 0:SEQ], scalar=B1[0:fn, one(layer(q)), 0, c],
                            in1=G1[0:fn, 0:SEQ], op0=ALU.add, op1=ALU.mult).then_inc(u_done, 1)
                    dve.wait_ge(po_mm, q + 1)
                    dve.wait_ge(ycb_ready, q + 1)
                    tt(Y[:, batch(q), :], M0t, YCB[:, :, :], ALU.add).then_inc(y_ready, 1)
                if b:
                    dve.wait_ge(p_ready, 2 * m + 2)
                    band(0, NWT - 1, 1, 0, 0, P)
                    for v in range(NWT):
                        last = band(1, v, 1, v, WIN, v * WIN)
                        if v < NWT - 1:
                            last = band(1, v, 1, v + 1, 0, (v + 1) * WIN)
                    last.then_inc(band_ready, 1)
                    dve.wait_ge(pj_mm, m + 1)
                    tt(YC[:, :, :], M0t, Y[:, batch(m), :], ALU.add).then_inc(yc_ready, 1)

            def band(kt, v, pt, w, j, c):
                return dve.transpose(BAND[kt][WIN * v:WIN * v + WIN, :, c:c + WIN],
                                     PB[WIN * w:WIN * w + WIN, pt, :, j:j + WIN])

            def scores(m, t):
                dve.wait_ge(sims_mm, 2 * m + t + 1)
                s = PB[:, t, :, :]
                for a in range(2):
                    last = tt(PB[:, t, a * BLK:(a + 1) * BLK, :], SP[a][:, :, :],
                              wide(mask[:, t:t + 1, :], 1, BLK), ALU.add)
                last.then_inc(s_masked, 1)
                dve.wait_ge(s_masked, 2 * m + t + 1)
                dve.tensor_reduce(MX[:, :], s, AX_X, ALU.max).then_inc(s_max, 1)
                dve.wait_ge(s_max, 2 * m + t + 1)
                tt(s, s, wide(MX[:, :].rearrange("p (h a) -> p h a", a=1), 2, 2 * WIN),
                   ALU.subtract).then_inc(s_shifted, 1)

            def sums(m, t):
                dve.wait_ge(p_exp, 2 * m + t + 1)
                dve.tensor_reduce(SS[:, :], PB[:, t, :, :], AX_X, ALU.add).then_inc(p_sum, 1)
                dve.wait_ge(p_sum, 2 * m + t + 1)
                dve.reciprocal(RS[:, t, :], SS[:, :]).then_inc(p_rsum, 1)

            def rope(n, t):
                for c in range(4):
                    h = c // 2
                    dve.wait_ge(sq_done, 8 * n + 4 * t + c + 1)
                    if c % 2 == 0:
                        after(dve, t2_used, 4 * n + 2 * t + h - 1)
                    raw = KB[c % 2][:, :]
                    cols = slice((c % 2) * CH, (c % 2 + 1) * CH)
                    tab = slice((t * 2 + h) * DH, (t * 2 + h + 1) * DH)
                    tt(T1[:, t, h, cols].rearrange("p (k d) -> p k d", k=HPC), raw.rearrange("p (k d) -> p k d", k=HPC),
                       wide(TA[:, one(layer(n)), tab], 1, HPC), ALU.mult)
                    for s in range(2):
                        last = tt(T2[:, h, cols].rearrange("p (k s d) -> p k s d", k=HPC, s=2)[:, :, s, :],
                                  raw.rearrange("p (k s d) -> p k s d", k=HPC, s=2)[:, :, 1 - s, :],
                                  wide(TB[:, one(layer(n)), tab.start + s * HALF:tab.start + (s + 1) * HALF], 1, HPC),
                                  ALU.mult)
                    last.then_inc(rope_done, 1)
                    dve.tensor_reduce(SSQ[:, t, h, (c % 2) * HPC:(c % 2 + 1) * HPC],
                                      SQ[:, c % 2, :].rearrange("p (k d) -> p k d", k=HPC), AX_X, ALU.add
                                      ).then_inc(sq_summed, 1)

            pipeline(dve, step)
            dve.wait_ge(y_ready, NB + NBL)
            stt(out=Y[:, :, :], in0=Y[:, :, :], scalar=tg[:, 1:2], in1=X1[:, :, :],
                op0=ALU.mult, op1=ALU.add).then_inc(o_ready, 1)

        @block.gpsimd
        def _(pool):
            tt, ts = pool.tensor_tensor, pool.tensor_scalar
            pool.memset(negh[:, :], -0.5).then_inc(zeroed, 1)
            pool.wait_ge(zeroed, 3)

            def power(mv, k, eps_done, rv):
                pool.wait_ge(mv, k + 1)
                apart(pool)
                ts(RV[:, :], MV[:, :, 1], EPS, None, ALU.add).then_inc(eps_done, 1)
                pool.wait_ge(eps_done, k + 1)
                tt(RV[:, :], RV[:, :], negh[:, 0:TILES], ALU.pow).then_inc(rv, 1)

            with pool.Fori(0, 2 * NB, 1) as k:
                power(f_mv, k, f_eps, f_rv)
            for i in range(2):
                last = pool.memset(BAND[i][:, :, :], 0.0)
            last.then_inc(zeroed, 1)

            def step(n, odd, a, b, d):
                m, q = n - 1, n - 2
                if d:
                    pool.wait_ge(yc_ready, q + 1)
                    apart(pool)
                    ts(XS[:, :, 0:D // 2], YC[:, :, 0:D // 2], 0.0, None, ALU.add).then_inc(xs_lo, 1)
                    pool.wait_ge(small_in, 16 * 4)
                    tt(YCB[:, :, :], YC[:, :, :], wide(B2[:, one(layer(q)), :], 1, TILES),
                       ALU.add).then_inc(ycb_ready, 1)
                    power(mv_done, q, var_eps, rv_done)
                if b:
                    norm(m, 0)
                if a:
                    unit(n, 0)
                if b:
                    norm(m, 1)
                if a:
                    unit(n, 1)

            def norm(m, t):
                pool.wait_ge(p_rsum, 2 * m + t + 1)
                tt(PB[:, t, :, :], PB[:, t, :, :],
                   wide(RS[:, t, :].rearrange("p (h a) -> p h a", a=1), 2, 2 * WIN), ALU.mult).then_inc(p_ready, 1)

            def unit(n, t):
                for h in range(2):
                    k = 4 * n + 2 * t + h
                    pool.wait_ge(sq_summed, 8 * n + 4 * t + 2 * h + 2)
                    apart(pool)
                    ts(RN[:, h, :], SSQ[:, t, h, :], 1e-24, None, ALU.max).then_inc(ss_clamped, 1)
                    pool.wait_ge(ss_clamped, k + 1)
                    tt(RN[:, h, :], RN[:, h, :], negh[:, :], ALU.pow).then_inc(rnorm, 1)
                    tt(T1[:, t, h, :], T1[:, t, h, :], T2[:, h, :], ALU.add).then_inc(t2_used, 1)
                    pool.wait_ge(rnorm, k + 1)
                    pool.wait_ge(t2_used, k + 1)
                    v = T1[:, t, h, :].rearrange("p (k d) -> p k d", k=HEADS)
                    tt(v, v, wide(RN[:, h, :].rearrange("p (h a) -> p h a", a=1), 2, DH),
                       ALU.mult).then_inc(t1_ready, 1)

            pipeline(pool, step)


_INS = ['x', 'ctx_1024', 'g_xattn', 'g_ffn', 'L0_ffn_Wqkv', 'L0_ffn_q_scale', 'L0_ffn_k_scale', 'L0_ffn_Wo',
        'L0_ffn_ln_g', 'L0_ffn_ln_b', 'L0_ffn_W1', 'L0_ffn_b1', 'L0_ffn_W2', 'L0_ffn_b2']


def constants():
    import numpy as np
    f = np.float32
    half = np.arange(0, DH, 2, dtype=f)
    inv_freq = (f(1.0) / f(10000.0) ** (half / f(DH))).astype(f)
    t = np.arange(SEQ, dtype=f)
    freqs = (t[:, None] * inv_freq[None, :]).astype(f)
    base = ((half + f(0.4 * DH)) / f(1.4 * DH)).astype(f)
    power = ((t - SEQ // 2) / f(WIN // 2)).astype(f)
    scale = (base[None, :] ** power[:, None]).astype(f)
    cos, sin = np.cos(freqs).astype(f), np.sin(freqs).astype(f)
    both = np.stack([scale, f(1.0) / scale], 1)
    cs = (cos[:, None, :] * both).astype(f)
    sn = (sin[:, None, :] * both).astype(f)
    cs = np.concatenate([cs, cs], -1)
    sn = np.concatenate([-sn, sn], -1)

    def lay(v):
        return np.ascontiguousarray(v.reshape(TILES, P, -1).transpose(1, 0, 2).reshape(P, -1))

    i, j = np.arange(WIN)[:, None], np.arange(2 * WIN)[None, :]
    seen = (i <= j) & (j <= i + WIN)
    m = np.where(seen, f(0), f(-1e30)).astype(f)
    m = np.tile(m, (SEQ // WIN, 1)).reshape(SEQ // WIN, WIN, 2 * WIN)
    m[0, :, 0:WIN] = -1e30
    return {
        'c_cos': lay(cs), 'c_sin': lay(sn), 'c_mask': lay(m.reshape(SEQ, 2 * WIN)),
        'c_ident': np.eye(P, dtype=f), 'c_shift': np.eye(P, k=1, dtype=f),
        'c_carry': (np.arange(P)[:, None] == P - 1).astype(f) * (np.arange(P)[None, :] == 0).astype(f),
    }


def arrays_of(inputs):
    import numpy as np
    a = {name: np.ascontiguousarray(inputs[name]) for name in _INS}
    for name in ('L0_ffn_ln_g', 'L0_ffn_ln_b'):
        a[name] = np.ascontiguousarray(a[name].T)
    b1 = np.zeros((P, DEPTH, 2, len(FC)), a['L0_ffn_b1'].dtype)
    for half in range(2):
        for c, (f0, fn) in enumerate(FC):
            b1[0:fn, :, half, c] = a['L0_ffn_b1'][:, half * FF + f0:half * FF + f0 + fn].T
    a['L0_ffn_b1'] = b1.reshape(P, -1)
    return a | constants()


def kernel(**inputs):
    import concourse.bacc as bacc
    from concourse.bass_utils import run_bass_kernel_spmd

    nc = bacc.Bacc("TRN2", target_bir_lowering=False, num_devices=1)
    arrays = arrays_of(inputs)
    args = [nc.dram_tensor(f"in_{k}", a.shape, mybir.dt.from_np(a.dtype), kind="ExternalInput").ap()
            for k, a in arrays.items()]
    args.append(nc.dram_tensor("out", (NB, SEQ, D), F32, kind="ExternalOutput").ap())
    flamingo_kernel(nc, *args)
    r = run_bass_kernel_spmd(nc, [{f"in_{k}": a for k, a in arrays.items()}], core_ids=[0])
    return r.results[0]["out"]
```

```python
from contextlib import ExitStack

import concourse.bass as bass
from concourse import mybir

F32 = mybir.dt.float32
ALU = mybir.AluOpType
ACT = mybir.ActivationFunctionType
AX_X = mybir.AxisListType.X

P = 128
NB = 8
SEQ = 256
TILES = SEQ // P
D = 128
DEPTH = 6
HEADS = 16
DH = 64
HALF = DH // 2
WIN = 32
NWT = P // WIN
INNER = HEADS * DH
BLK = INNER // P
FF = int(D * 4 * 2 / 3)
FC = [(0, 128), (128, 128), (256, FF - 256)]
CH = 512
HPC = CH // DH
NBL = NB * DEPTH
EPS = 1e-5
QK_SCALE = 8.0
BANDW = P + WIN
CHUNKS = [(0, 0), (0, 1), (0, 2), (0, 3), (0, 4), (0, 5), (1, 4), (1, 5), (1, 0), (1, 1), (1, 2), (1, 3)]
PARTS = [(0, 12), (12, 16)]


def flamingo_kernel(nc, x, ctx, g_xattn, g_ffn, wqkv, q_scale, k_scale, wo, ln_g, ln_b, w1, b1, w2, b2,
                    c_cos, c_sin, c_mask, c_ident, c_shift, c_carry, out):
    x_v = x.rearrange("b (t p) d -> p (b t) d", p=P)
    ctx_v = ctx.rearrange("b (t p) d -> p (b t) d", p=P)
    out_v = out.rearrange("b (t p) d -> p (b t) d", p=P)

    with ExitStack() as es:
        def sb(name, shape):
            return es.enter_context(nc.sbuf_tensor(name, shape, F32))

        def bank(name, shape):
            return es.enter_context(nc.psum_tensor(name, shape, F32))

        def sem(name):
            return es.enter_context(nc.semaphore(name))

        Wqkv = sb("Wqkv", [P, 2, 3 * INNER])
        Wo = sb("Wo", [P, 2, BLK, D])
        W1 = sb("W1", [P, DEPTH, 2 * FF])
        W1c = sb("W1c", [P, 2 * FF])
        W2 = sb("W2", [P, DEPTH, len(FC), D])
        B1 = sb("B1", [P, DEPTH, 2, len(FC)])
        B2 = sb("B2", [P, DEPTH, D])
        G = sb("G", [P, DEPTH])
        Bt = sb("Bt", [P, DEPTH])
        TA = sb("TA", [P, DEPTH, TILES * 2 * DH])
        TB = sb("TB", [P, DEPTH, TILES * 2 * DH])
        cosc = sb("cosc", [P, TILES * 2 * DH])
        sinc = sb("sinc", [P, TILES * 2 * DH])
        mask = sb("mask", [P, TILES, 2 * WIN])
        ident = sb("ident", [P, P])
        shift = sb("shift", [P, P])
        carry = sb("carry", [P, P])
        negh = sb("negh", [P, HEADS])
        gates = sb("gates", [P, 2])
        tg = sb("tg", [P, 2])
        X1 = sb("X1", [P, NB * TILES, D])
        Y = sb("Y", [P, NB * TILES, D])
        YA = sb("YA", [P, TILES, D])
        YT = sb("YT", [P, SEQ])
        SQ = sb("SQ", [P, 2, CH])
        SSQ = sb("SSQ", [P, TILES, 2, HEADS])
        RK = sb("RK", [P, HEADS])
        RQ = sb("RQ", [P, 2, TILES, HEADS])
        T1 = sb("T1", [P, TILES, 2, INNER])
        T2q = sb("T2q", [P, TILES, INNER])
        T2k = sb("T2k", [P, INNER])
        QT = sb("QT", [P, BLK, SEQ])
        KT = sb("KT", [P, BLK, WIN + SEQ])
        V = sb("V", [P, 2, TILES, INNER])
        PB = sb("PB", [P, TILES, HEADS, 2 * WIN])
        NMX = sb("NMX", [P, TILES, HEADS])
        SS = sb("SS", [P, TILES, HEADS])
        RS = sb("RS", [P, TILES, HEADS])
        BAND = [sb("BAND0", [P, HEADS, BANDW]), sb("BAND1", [P, HEADS, P])]
        OTS = sb("OTS", [P, BLK, SEQ])
        YC = sb("YC", [P, TILES, D])
        YCB = sb("YCB", [P, TILES, D])
        XS = sb("XS", [P, TILES, D])
        XN = sb("XN", [P, TILES, D])
        XNT = sb("XNT", [P, SEQ])
        BS = sb("BS", [P, TILES, 6])
        MV = sb("MV", [P, TILES, 2])
        RV = sb("RV", [P, TILES])
        BSa = sb("BSa", [P, NB * TILES, 6])
        MVa = sb("MVa", [P, NB * TILES, 2])
        RVa = sb("RVa", [P, NB * TILES])
        G1 = sb("G1", [P, 2 * SEQ])
        U = sb("U", [P, len(FC), SEQ])
        CTX = T2q[:, :, :].rearrange("p a n -> p (a n)").rearrange("p (k d) -> p k d", d=D)
        QS = QT[:, 0:3, :].rearrange("p a n -> p (a n)").rearrange("p (l n) -> p l n", l=DEPTH)
        XNs = [XN, XS]
        CTs = [YC, YCB]
        XCT = [OTS[:, 2 * i:2 * i + 2, :].rearrange("p a n -> p (a n)") for i in range(2)]
        Us = [OTS[:, 4 + 2 * i:6 + 2 * i, :].rearrange("p a n -> p (a n)") for i in range(2)]
        Gs = [PB[:, i, 0:HPC, :].rearrange("p h n -> p (h n)") for i in range(2)]

        KB = [bank(f"KB{i}", [P, CH]) for i in range(2)]
        TQ = [bank(f"TQ{i}", [P, CH]) for i in range(2)]
        SP = [bank(f"SP{i}", [P, BLK, 2 * WIN]) for i in range(2)]
        FP = [sp[:, :, :].rearrange("p k n -> p (k n)") for sp in SP]
        M0 = bank("M0", [P, CH])
        M1 = bank("M1", [P, CH])
        M0t = M0[:, 0:TILES * D].rearrange("p (t d) -> p t d", t=TILES)

        x_in = sem("x_in")
        ctx_in = sem("ctx_in")
        const_in = sem("const_in")
        scale_in = sem("scale_in")
        small_in = sem("small_in")
        ffn_in = sem("ffn_in")
        wqkv_in = sem("wqkv_in")
        wo_in = sem("wo_in")
        zeroed = sem("zeroed")
        tanh_done = sem("tanh_done")
        tab_done = sem("tab_done")
        f_stats = sem("f_stats")
        f_mv = sem("f_mv")
        f_eps = sem("f_eps")
        f_rv = sem("f_rv")
        f_xn = sem("f_xn")
        f_cts = sem("f_cts")
        f_tr = sem("f_tr")
        f_ev = sem("f_ev")
        f_h = sem("f_h")
        f_gelu = sem("f_gelu")
        f_u = sem("f_u")
        f_o = sem("f_o")
        f_x1 = sem("f_x1")
        ya_copied = sem("ya_copied")
        xt_mm = sem("xt_mm")
        yt_ready = sem("yt_ready")
        chunk_mm = sem("chunk_mm")
        v_evac = sem("v_evac")
        sq_done = sem("sq_done")
        rope_done = sem("rope_done")
        sq_summed = sem("sq_summed")
        k_added = sem("k_added")
        ss_clamped = sem("ss_clamped")
        rq_ready = sem("rq_ready")
        rk_ready = sem("rk_ready")
        q_ready = sem("q_ready")
        k_ready = sem("k_ready")
        tq_mm = sem("tq_mm")
        tq_evac = sem("tq_evac")
        ot_mm = sem("ot_mm")
        ot_evac = sem("ot_evac")
        sims_mm = sem("sims_mm")
        s_masked = sem("s_masked")
        s_max = sem("s_max")
        s_shifted = sem("s_shifted")
        p_exp = sem("p_exp")
        p_rsum = sem("p_rsum")
        p_ready = sem("p_ready")
        band_ready = sem("band_ready")
        pj_mm = sem("pj_mm")
        yc_ready = sem("yc_ready")
        fx_mm = sem("fx_mm")
        xs_hi = sem("xs_hi")
        xs_lo = sem("xs_lo")
        ycb_ready = sem("ycb_ready")
        bn_done = sem("bn_done")
        mv_done = sem("mv_done")
        var_eps = sem("var_eps")
        rv_done = sem("rv_done")
        xn_ready = sem("xn_ready")
        ft_mm = sem("ft_mm")
        xnt_ready = sem("xnt_ready")
        w1c_ready = sem("w1c_ready")
        h_mm = sem("h_mm")
        g_ready = sem("g_ready")
        u_done = sem("u_done")
        po_mm = sem("po_mm")
        y_ready = sem("y_ready")
        o_ready = sem("o_ready")
        out_done = sem("out_done")
        waited = sem("waited")

        def wide(ap, dim, n):
            shape = list(ap.shape)
            shape[dim] = n
            return ap.broadcast_to(shape)

        def batch(n):
            return bass.ds((n & (NB - 1)) * TILES, TILES)

        def layer(n):
            if isinstance(n, int):
                return n // NB
            return nc.s_assert_within(n // NB, 0, DEPTH - 1,
                                      skip_runtime_bounds_check_because="steps end before NBL = NB * DEPTH")

        def one(i):
            return bass.ds(i, 1)

        def after(eng, s, count):
            if not isinstance(count, int) or count > 0:
                eng.wait_ge(s, count)

        def apart(eng):
            eng.sem_inc(waited, 1)

        def pipeline(eng, step, steps, depth):
            def at(n):
                return [0 <= n - k < steps for k in range(depth + 1)]

            first = depth + depth % 2
            for n in range(first):
                step(n, n % 2, *at(n))
            with eng.Fori(first, steps, 2) as i:
                step(i, 0, *[True] * (depth + 1))
                step(i + 1, 1, *[True] * (depth + 1))
            for n in range(steps, steps + depth):
                step(n, n % 2, *at(n))

        block = es.enter_context(nc.Block())

        @block.sync
        def _(sp):
            sp.dma_start(X1[:, :, :], x_v).then_inc(x_in, 16)
            sp.dma_start(CTX, ctx_v).then_inc(ctx_in, 16)
            sp.dma_start(ident[:, :], c_ident).then_inc(const_in, 16)
            sp.dma_start(shift[:, :], c_shift).then_inc(const_in, 16)
            sp.dma_start(carry[:, :], c_carry).then_inc(const_in, 16)
            sp.dma_start(cosc[:, :], c_cos).then_inc(const_in, 16)
            sp.dma_start(sinc[:, :], c_sin).then_inc(const_in, 16)
            sp.dma_start(mask[:, :, :].rearrange("p t n -> p (t n)"), c_mask).then_inc(const_in, 16)
            sp.dma_start(gates[:, 0:1], wide(g_xattn.rearrange("(a n) -> a n", a=1), 0, P)).then_inc(const_in, 16)
            sp.dma_start(gates[:, 1:2], wide(g_ffn.rearrange("(a n) -> a n", a=1), 0, P)).then_inc(const_in, 16)
            for l in range(DEPTH):
                sp.dma_start(QS[:, l, 0:DH], wide(q_scale[l:l + 1, :], 0, P)).then_inc(scale_in, 16)
                sp.dma_start(QS[:, l, DH:2 * DH], wide(k_scale[l:l + 1, :], 0, P)).then_inc(scale_in, 16)
            sp.dma_start(W1[:, :, :], w1.rearrange("l d n -> d l n")).then_inc(ffn_in, 16)
            for c, (f0, fn) in enumerate(FC):
                sp.dma_start(W2[0:fn, :, c, :], w2[:, f0:f0 + fn, :].rearrange("l f d -> f l d")).then_inc(ffn_in, 16)
            sp.dma_start(B2[:, :, :], wide(b2.rearrange("(a l) d -> a l d", a=1), 0, P)).then_inc(small_in, 16)
            sp.dma_start(G[:, :], ln_g).then_inc(small_in, 16)
            sp.dma_start(Bt[:, :], ln_b).then_inc(small_in, 16)
            sp.dma_start(B1[:, :, :, :].rearrange("p l h c -> p (l h c)"), b1).then_inc(small_in, 16)

            def load_layer(l, slot):
                sp.dma_start(Wqkv[:, one(slot), :].rearrange("p a n -> p (a n)"),
                             wqkv[one(l), :, :].rearrange("a d n -> (a d) n")).then_inc(wqkv_in, 16)
                sp.dma_start(Wo[:, one(slot), :, :].rearrange("p a k d -> p (a k) d"),
                             wo[one(l), :, :].rearrange("a (k p) d -> p (a k) d", p=P)).then_inc(wo_in, 16)

            load_layer(0, 0)
            sp.wait_ge(wqkv_in, 16)
            sp.wait_ge(wo_in, 16)
            load_layer(1, 1)
            with sp.Fori(2, DEPTH, 1) as l:
                sp.wait_ge(wqkv_in, 16 * l)
                sp.wait_ge(wo_in, 16 * l)
                sp.wait_ge(pj_mm, (l - 1) * NB)
                apart(sp)
                load_layer(l, l & 1)
            for i, (t0, t1) in enumerate(PARTS):
                sp.wait_ge(o_ready, i + 1)
                sp.dma_start(out_v[:, t0:t1, :], Y[:, t0:t1, :]).then_inc(out_done, 16)
            sp.wait_ge(out_done, 16 * len(PARTS))

        @block.tensor
        def _(pe):
            mm, tr = pe.matmul, pe.transpose

            def first(n, odd, a, b, c):
                if c:
                    pe.wait_ge(f_u, n - 1)
                    after(pe, f_x1, n - 2)
                    for t in range(TILES):
                        for f in range(TILES):
                            last = mm(KB[odd][:, t * D:(t + 1) * D],
                                      Us[odd][:, f * SEQ + t * P:f * SEQ + (t + 1) * P], CTs[odd][:, f, :],
                                      start=(f == 0), stop=(f == TILES - 1))
                    last.then_inc(f_o, 1)
                if a:
                    pe.wait_ge(f_xn, n + 1)
                    pe.wait_ge(f_cts, n + 1)
                    after(pe, f_ev, n - 1)
                    for t in range(TILES):
                        tr(TQ[odd][:, t * P:(t + 1) * P], XNs[odd][:, t, :], ident[:, :])
                        last = tr(TQ[odd][:, SEQ + t * P:SEQ + (t + 1) * P], CTs[odd][:, t, :], ident[:, :])
                    last.then_inc(f_tr, 1)
                if b:
                    pe.wait_ge(f_ev, n)
                    after(pe, f_u, n - 2)
                    xct = XCT[1 - odd]
                    for f in range(TILES):
                        last = mm(FP[1 - odd][:, f * SEQ:(f + 1) * SEQ], xct[:, SEQ + f * P:SEQ + (f + 1) * P],
                                  xct[:, 0:SEQ], start=True, stop=True)
                    last.then_inc(f_h, 1)

            pe.wait_ge(const_in, 16 * 8)
            pipeline(pe, first, NB, 2)
            pe.wait_ge(f_x1, NB)

            def step(n, odd, a, b, c, d):
                if b:
                    turn(n - 1, 0)
                if a:
                    pe.wait_ge(ya_copied, n + 1)
                    if d:
                        after(pe, u_done, 3 * (n - 3))
                    for t in range(TILES):
                        last = tr(M1[:, t * P:(t + 1) * P], YA[:, t, :], ident[:, :])
                    last.then_inc(xt_mm, 1)
                if b:
                    sims(n - 1, 0)
                    turn(n - 1, 1)
                if a:
                    qkv(n, (0, 1))
                if d:
                    if a:
                        pe.wait_ge(yt_ready, n + 1)
                    else:
                        pe.wait_ge(u_done, 3 * (n - 3))
                    pe.wait_ge(yc_ready, n - 2)
                    fx = M1[:, 0:TILES * HALF * 2].rearrange("p (t d) -> p t d", t=TILES)
                    mm(fx, shift[:, :], YC[:, :, D // 2:D], start=True, stop=False, skip_group_check=True)
                    mm(fx[:, 1, :], carry[:, :], YC[:, 0, D // 2:D], start=False, stop=True,
                       skip_group_check=True).then_inc(fx_mm, 1)
                if b:
                    sims(n - 1, 1)
                for k in range(4):
                    if a and k < 2:
                        qkv(n, (k + 2,))
                    if c:
                        attend(n - 2, odd, b, k)
                if a:
                    qkv(n, range(4, 8))
                if d:
                    pe.wait_ge(xn_ready, n - 2)
                    for t in range(TILES):
                        last = tr(M1[:, t * P:(t + 1) * P], XN[:, t, :], ident[:, :])
                    last.then_inc(ft_mm, 1)
                for k in range(len(FC)):
                    if a:
                        qkv(n, (k + 8,))
                    if d:
                        ffn_in_mm(n - 3, k)
                if c:
                    project(n - 2, d)
                if a:
                    qkv(n, (11,))
                if d:
                    ffn_out_mm(n - 3, c)

            def qkv(n, which):
                for i in which:
                    t, c = CHUNKS[i]
                    if i == 0:
                        pe.wait_ge(yt_ready, n + 1)
                        pe.wait_ge(wqkv_in, 16 * (layer(n) + 1))
                    if i < 2:
                        after(pe, rope_done, 8 * n - 1 + i)
                    elif i < 6:
                        pe.wait_ge(rope_done, 8 * n + i - 1)
                    elif i < 10:
                        pe.wait_ge(v_evac, 4 * n + i - 5)
                    else:
                        pe.wait_ge(rope_done, 8 * n + i - 5)
                    mm(KB[i % 2][:, :], YT[:, t * P:(t + 1) * P],
                       Wqkv[:, one(layer(n) & 1), c * CH:(c + 1) * CH].rearrange("p a n -> p (a n)"),
                       start=True, stop=True).then_inc(chunk_mm, 1)

            def turn(m, t):
                for g in range(4):
                    pe.wait_ge((q_ready, k_ready)[g // 2], 4 * m + 2 * t + g % 2 + 1)
                    if t == 0 and g < 2:
                        after(pe, ot_evac, 4 * (m - 2) + 3 + g)
                    else:
                        pe.wait_ge(tq_evac, 8 * m + 4 * t + g - 1)
                    for k in range(4):
                        c = (g % 2) * CH + k * P
                        last = tr(TQ[g % 2][:, k * P:(k + 1) * P], T1[:, t, g // 2, c:c + P], ident[:, :])
                    last.then_inc(tq_mm, 1)

            def sims(m, t):
                pe.wait_ge(tq_evac, 8 * m + 4 * t + 4)
                after(pe, s_masked, 2 * m + t)
                apart(pe)
                for blk in range(BLK):
                    for w in range(NWT):
                        for a in range(2):
                            rows = slice(DH * a, DH * a + DH)
                            c = t * P + w * WIN
                            last = mm(SP[a][WIN * w:WIN * w + WIN, blk, :], QT[rows, blk, c:c + WIN],
                                      KT[rows, blk, c:c + 2 * WIN], start=True, stop=True)
                last.then_inc(sims_mm, 1)

            def attend(m, odd, turned, k):
                if k == 0:
                    pe.wait_ge(band_ready, m + 1)
                    pe.wait_ge(v_evac, 4 * m + 4)
                if k >= 2:
                    pe.wait_ge(ot_evac, 4 * m + k - 1)
                elif turned:
                    pe.wait_ge(tq_evac, 8 * m + 15 + k)
                for i in range(2):
                    blk = 2 * k + i
                    for a in range(2):
                        h = 2 * blk + a
                        o = TQ[k % 2][DH * a:DH * a + DH, i * SEQ:(i + 1) * SEQ]
                        mm(o[:, P:SEQ], V[:, odd, 1, h * DH:(h + 1) * DH], BAND[1][:, a * BLK + blk, :],
                           start=True, stop=False, skip_group_check=True)
                        last = mm(o[:, 0:BANDW], V[:, odd, 0, h * DH:(h + 1) * DH], BAND[0][:, a * BLK + blk, :],
                                  start=False, stop=True, skip_group_check=True)
                last.then_inc(ot_mm, 1)

            def project(m, d):
                pe.wait_ge(ot_evac, 4 * m + 4)
                if d:
                    pe.wait_ge(y_ready, NB + m - 1)
                pe.wait_ge(wo_in, 16 * (layer(m) + 1))
                for t in range(TILES):
                    for blk in range(BLK):
                        last = mm(M0t[:, t, :], OTS[:, blk, t * P:(t + 1) * P],
                                  Wo[:, one(layer(m) & 1), blk, :].rearrange("p a d -> p (a d)"),
                                  start=(blk == 0), stop=(blk == BLK - 1))
                last.then_inc(pj_mm, 1)

            def ffn_in_mm(q, c):
                f0, fn = FC[c]
                pe.wait_ge(xnt_ready, q + 1)
                pe.wait_ge(w1c_ready, q + 1)
                after(pe, u_done, 3 * q + c)
                for half in range(2):
                    last = mm(M1[0:fn, half * SEQ:(half + 1) * SEQ],
                              W1c[:, half * FF + f0:half * FF + f0 + fn], XNT[:, :], start=True, stop=True)
                last.then_inc(h_mm, 1)

            def ffn_out_mm(q, c):
                pe.wait_ge(u_done, 3 * q + 3)
                if c:
                    pe.wait_ge(yc_ready, q + 2)
                for t in range(TILES):
                    for k, (f0, fn) in enumerate(FC):
                        last = mm(M0t[:, t, :], U[0:fn, k, t * P:(t + 1) * P],
                                  W2[0:fn, one(layer(q)), k, :].rearrange("p a d -> p (a d)"),
                                  start=(k == 0), stop=(k == len(FC) - 1))
                last.then_inc(po_mm, 1)

            pipeline(pe, step, NBL, 3)

        @block.scalar
        def _(act):
            f = act.activation
            act.wait_ge(const_in, 16 * 8)
            f(tg[:, :], gates[:, :], ACT.Tanh).then_inc(tanh_done, 1)
            act.wait_ge(ctx_in, 16)

            def first(n, odd, a, b, c):
                if a:
                    after(act, f_o, n - 1)
                    f(CTs[odd][:, :, :], CTX[:, batch(n), :], ACT.Copy).then_inc(f_cts, 1)
                    act.wait_ge(f_tr, n + 1)
                    f(XCT[odd], TQ[odd][:, :], ACT.Copy).then_inc(f_ev, 1)
                if b:
                    act.wait_ge(f_h, n)
                    f(Gs[1 - odd], FP[1 - odd], ACT.Gelu).then_inc(f_gelu, 1)

            pipeline(act, first, NB, 2)

            def step(n, odd, a, b, c, d):
                q = n - 3
                if a:
                    act.wait_ge(y_ready, n + 1)
                    after(act, xt_mm, n)
                    f(YA[:, :, :], Y[:, batch(n), :], ACT.Copy).then_inc(ya_copied, 1)
                if b:
                    evac_turned(n - 1, 0)
                if a:
                    act.wait_ge(xt_mm, n + 1)
                    f(YT[0:D // 2, :], M1[0:D // 2, 0:SEQ], ACT.Copy)
                    f(YT[D // 2:D, 1:SEQ], M1[D // 2:D, 0:SEQ - 1], ACT.Copy).then_inc(yt_ready, 1)
                if b:
                    evac_turned(n - 1, 1)
                if a:
                    square(n, 0, 0)
                    square(n, 0, 1)
                if d:
                    act.wait_ge(fx_mm, q + 1)
                    f(XS[:, :, D // 2:D], M1[:, 0:TILES * D // 2].rearrange("p (t d) -> p t d", t=TILES),
                      ACT.Copy).then_inc(xs_hi, 1)
                if b:
                    exps(n - 1, 0, 1 - odd, 0)
                    exps(n - 1, 0, 1 - odd, 1)
                for k in range(2):
                    if a:
                        square(n, 0, k + 2)
                    if c:
                        evac_o(n - 2, k)
                if b:
                    exps(n - 1, 1, 1 - odd, 0)
                if c:
                    evac_o(n - 2, 2)
                    evac_o(n - 2, 3)
                if a:
                    evac_v(n, 0, odd, 0)
                    evac_v(n, 0, odd, 1)
                if b:
                    exps(n - 1, 1, 1 - odd, 1)
                if a:
                    evac_v(n, 1, odd, 0)
                    evac_v(n, 1, odd, 1)
                if d:
                    after(act, h_mm, 3 * q)
                    act.wait_ge(ffn_in, 16 * 4)
                    f(W1c[:, :], W1[:, one(layer(q)), :].rearrange("p a n -> p (a n)"), ACT.Copy).then_inc(w1c_ready, 1)
                if d:
                    act.wait_ge(ft_mm, q + 1)
                    act.wait_ge(small_in, 16 * 4)
                    f(XNT[:, :], M1[:, 0:SEQ], ACT.Identity, bias=Bt[:, one(layer(q))],
                      scale=G[:, one(layer(q))]).then_inc(xnt_ready, 1)
                for k in range(len(FC)):
                    if a:
                        square(n, 1, k)
                    if d:
                        fn = FC[k][1]
                        act.wait_ge(h_mm, 3 * q + k + 1)
                        f(G1[0:fn, 0:SEQ], M1[0:fn, SEQ:2 * SEQ], ACT.Gelu,
                          bias=B1[0:fn, one(layer(q)), 1, k]).then_inc(g_ready, 1)
                if a:
                    square(n, 1, 3)

            def evac_o(m, k):
                act.wait_ge(ot_mm, 4 * m + k + 1)
                f(OTS[:, 2 * k:2 * k + 2, :], TQ[k % 2][:, :].rearrange("p (k n) -> p k n", k=2),
                  ACT.Copy).then_inc(ot_evac, 1)

            def evac_turned(m, t):
                for g in range(4):
                    act.wait_ge(tq_mm, 8 * m + 4 * t + g + 1)
                    to, c0 = (QT, t * P) if g < 2 else (KT, WIN + t * P)
                    f(to[:, 4 * (g % 2):4 * (g % 2) + 4, c0:c0 + P],
                      TQ[g % 2][:, :].rearrange("p (k n) -> p k n", k=4), ACT.Copy).then_inc(tq_evac, 1)

            def exps(m, t, odd, a):
                act.wait_ge(s_shifted, 2 * m + t + 1)
                for blk in range(BLK):
                    i, h = a * BLK + blk, 2 * blk + a
                    last = f(PB[:, t, i, :], PB[:, t, i, :], ACT.Exp, bias=NMX[:, t, i:i + 1],
                             scale=RQ[:, odd, t, h:h + 1], accum_out=SS[:, t, i:i + 1])
                if a:
                    last.then_inc(p_exp, 1)

            def evac_v(n, t, odd, j):
                act.wait_ge(chunk_mm, 12 * n + CHUNKS.index((t, 4 + j)) + 1)
                f(V[:, odd, t, j * CH:(j + 1) * CH], KB[j][:, :], ACT.Copy).then_inc(v_evac, 1)

            def square(n, t, c):
                act.wait_ge(chunk_mm, 12 * n + CHUNKS.index((t, c)) + 1)
                after(act, sq_summed, 8 * n + 4 * t + c - 1)
                f(SQ[:, c % 2, :], KB[c % 2][:, :], ACT.Square).then_inc(sq_done, 1)

            pipeline(act, step, NBL, 3)

        @block.vector
        def _(dve):
            tt, ts, stt = dve.tensor_tensor, dve.tensor_scalar, dve.scalar_tensor_tensor
            dve.memset(YT[D // 2:D, 0:1], 0.0).then_inc(zeroed, 1)
            dve.memset(KT[:, :, 0:WIN], 0.0).then_inc(zeroed, 1)

            def stats_all(k):
                with dve.Fori(0, NB * TILES, 1) as i:
                    last = dve.bn_stats(BSa[:, one(i), :].rearrange("p a n -> p (a n)"),
                                        X1[:, one(i), :].rearrange("p a n -> p (a n)"))
                    last.then_inc(f_stats, 1)
                dve.wait_ge(f_stats, (k + 1) * NB * TILES)
                for i in range(NB * TILES):
                    last = dve.bn_aggr(MVa[:, i, :], BSa[:, i, :])
                last.then_inc(f_mv, 1)
                dve.wait_ge(f_rv, k + 1)

            def normalize(to, i):
                return ts(to, X1[:, one(i), :].rearrange("p a d -> p (a d)"), MVa[:, one(i), 0], RVa[:, one(i)],
                          ALU.subtract, ALU.mult)

            def first(n, odd, a, b, c):
                if a:
                    after(dve, f_tr, n - 1)
                    for t in range(TILES):
                        last = normalize(XNs[odd][:, t, :], (n & (NB - 1)) * TILES + t)
                    last.then_inc(f_xn, 1)
                if c:
                    dve.wait_ge(f_o, n - 1)
                    stt(out=X1[:, batch(n - 2), :], in0=KB[odd][:, 0:TILES * D].rearrange("p (t d) -> p t d", t=TILES),
                        scalar=tg[:, 0:1], in1=X1[:, batch(n - 2), :], op0=ALU.mult, op1=ALU.add).then_inc(f_x1, 1)
                if b:
                    dve.wait_ge(f_gelu, n)
                    after(dve, f_o, n - 2)
                    tt(Us[1 - odd], FP[1 - odd], Gs[1 - odd], ALU.mult).then_inc(f_u, 1)

            dve.wait_ge(x_in, 16)
            stats_all(0)
            dve.wait_ge(tanh_done, 1)
            pipeline(dve, first, NB, 2)
            dve.wait_ge(f_x1, NB)
            stats_all(1)
            with dve.Fori(0, NB, 1) as b:
                for t in range(TILES):
                    last = normalize(Y[:, one(b * TILES + t), :].rearrange("p a d -> p (a d)"), b * TILES + t)
                last.then_inc(y_ready, 1)

            dve.wait_ge(scale_in, 16 * 2 * DEPTH)
            dve.wait_ge(const_in, 16 * 8)
            qs = QS[:, :, :].rearrange("p l (c s d) -> p l c s d", c=2, s=2)
            for l in range(DEPTH):
                for t in range(TILES):
                    cols = slice(t * 2 * DH, (t + 1) * 2 * DH)
                    tt(TA[:, l, cols], cosc[:, cols], QS[:, l, :], ALU.mult)
                    last = tt(TB[:, l, cols].rearrange("p (c s d) -> p c s d", c=2, s=2),
                              sinc[:, cols].rearrange("p (c s d) -> p c s d", c=2, s=2),
                              qs[:, l, :, ::-1, :], ALU.mult)
            last.then_inc(tab_done, 1)
            dve.wait_ge(tab_done, 1)

            def step(n, odd, a, b, c, d):
                m, q = n - 1, n - 3
                if b:
                    scores(m, 0, 1 - odd)
                if a:
                    rope(n, 0, (0, 1))
                if b:
                    scores(m, 1, 1 - odd)
                if d:
                    dve.wait_ge(xs_hi, q + 1)
                    dve.wait_ge(xs_lo, q + 1)
                    apart(dve)
                    for t in range(TILES):
                        last = dve.bn_stats(BS[:, t, :], XS[:, t, :])
                    last.then_inc(bn_done, 1)
                    dve.wait_ge(bn_done, q + 1)
                    apart(dve)
                    for t in range(TILES):
                        last = dve.bn_aggr(MV[:, t, :], BS[:, t, :])
                    last.then_inc(mv_done, 1)
                if b:
                    inverse_sums(m, 0)
                if a:
                    rope(n, 0, (2, 3))
                if d:
                    dve.wait_ge(rv_done, q + 1)
                    for t in range(TILES):
                        last = ts(XN[:, t, :], XS[:, t, :], MV[:, t, 0:1], RV[:, t:t + 1], ALU.subtract, ALU.mult)
                    last.then_inc(xn_ready, 1)
                if b:
                    dve.wait_ge(p_ready, 2 * m + 1)
                    after(dve, ot_mm, 4 * m)
                    dve.wait_ge(zeroed, 4)
                    for v in range(NWT):
                        band(0, v, 0, v, WIN, v * WIN)
                        if v < NWT - 1:
                            band(0, v, 0, v + 1, 0, (v + 1) * WIN)
                    inverse_sums(m, 1)
                for k, (f0, fn) in enumerate(FC):
                    if a:
                        rope(n, 1, (k,))
                    if d:
                        dve.wait_ge(g_ready, 3 * q + k + 1)
                        stt(out=U[0:fn, k, :], in0=M1[0:fn, 0:SEQ], scalar=B1[0:fn, one(layer(q)), 0, k],
                            in1=G1[0:fn, 0:SEQ], op0=ALU.add, op1=ALU.mult).then_inc(u_done, 1)
                if c:
                    dve.wait_ge(pj_mm, n - 1)
                    tt(YC[:, :, :], M0t, Y[:, batch(n - 2), :], ALU.add).then_inc(yc_ready, 1)
                if a:
                    rope(n, 1, (3,))
                if b:
                    dve.wait_ge(p_ready, 2 * m + 2)
                    band(0, NWT - 1, 1, 0, 0, P)
                    for v in range(NWT):
                        last = band(1, v, 1, v, WIN, v * WIN)
                        if v < NWT - 1:
                            last = band(1, v, 1, v + 1, 0, (v + 1) * WIN)
                    last.then_inc(band_ready, 1)
                if d:
                    dve.wait_ge(po_mm, q + 1)
                    dve.wait_ge(ycb_ready, q + 1)
                    tt(Y[:, batch(q), :], M0t, YCB[:, :, :], ALU.add).then_inc(y_ready, 1)
                if not a and n - 2 < NBL <= n - 1:
                    finish(0)

            def finish(i):
                t0, t1 = PARTS[i]
                dve.wait_ge(y_ready, NBL + t1 // TILES)
                stt(out=Y[:, t0:t1, :], in0=Y[:, t0:t1, :], scalar=tg[:, 1:2], in1=X1[:, t0:t1, :],
                    op0=ALU.mult, op1=ALU.add).then_inc(o_ready, 1)

            def band(kt, v, pt, w, j, c):
                return dve.transpose(BAND[kt][WIN * v:WIN * v + WIN, :, c:c + WIN],
                                     PB[WIN * w:WIN * w + WIN, pt, :, j:j + WIN])

            def scores(m, t, odd):
                dve.wait_ge(sims_mm, 2 * m + t + 1)
                for a in range(2):
                    last = tt(PB[:, t, a * BLK:(a + 1) * BLK, :], SP[a][:, :, :],
                              wide(mask[:, t:t + 1, :], 1, BLK), ALU.add)
                last.then_inc(s_masked, 1)
                dve.wait_ge(s_masked, 2 * m + t + 1)
                dve.tensor_reduce(NMX[:, t, :], PB[:, t, :, :], AX_X, ALU.max).then_inc(s_max, 1)
                dve.wait_ge(s_max, 2 * m + t + 1)
                dve.wait_ge(rq_ready, 4 * m + 2 * t + 2)
                nmx = NMX[:, t, :].rearrange("p (a k) -> p a k", a=2)
                stt(out=nmx, in0=nmx, scalar=-1.0, in1=RQ[:, odd, t, :].rearrange("p (k a) -> p a k", a=2),
                    op0=ALU.mult, op1=ALU.mult).then_inc(s_shifted, 1)

            def inverse_sums(m, t):
                dve.wait_ge(p_exp, 2 * m + t + 1)
                dve.reciprocal(RS[:, t, :], SS[:, t, :]).then_inc(p_rsum, 1)

            def rope(n, t, which):
                for c in which:
                    h = c // 2
                    dve.wait_ge(sq_done, 8 * n + 4 * t + c + 1)
                    if c < 2:
                        after(dve, q_ready, 4 * n + 2 * t - 3 + c)
                    else:
                        after(dve, k_added, 4 * n + 2 * t - 3 + c)
                    t2 = T2k[:, :] if h else T2q[:, t, :]
                    raw = KB[c % 2][:, :]
                    cols = slice((c % 2) * CH, (c % 2 + 1) * CH)
                    tab = slice((t * 2 + h) * DH, (t * 2 + h + 1) * DH)
                    tt(T1[:, t, h, cols].rearrange("p (k d) -> p k d", k=HPC), raw.rearrange("p (k d) -> p k d", k=HPC),
                       wide(TA[:, one(layer(n)), tab], 1, HPC), ALU.mult)
                    for s in range(2):
                        last = tt(t2[:, cols].rearrange("p (k s d) -> p k s d", k=HPC, s=2)[:, :, s, :],
                                  raw.rearrange("p (k s d) -> p k s d", k=HPC, s=2)[:, :, 1 - s, :],
                                  wide(TB[:, one(layer(n)), tab.start + s * HALF:tab.start + (s + 1) * HALF], 1, HPC),
                                  ALU.mult)
                    last.then_inc(rope_done, 1)
                    dve.tensor_reduce(SSQ[:, t, h, (c % 2) * HPC:(c % 2 + 1) * HPC],
                                      SQ[:, c % 2, :].rearrange("p (k d) -> p k d", k=HPC), AX_X, ALU.add
                                      ).then_inc(sq_summed, 1)

            pipeline(dve, step, NBL, 3)
            finish(1)

        @block.gpsimd
        def _(pool):
            tt, ts = pool.tensor_tensor, pool.tensor_scalar
            pool.memset(negh[:, :], -0.5).then_inc(zeroed, 1)
            pool.wait_ge(zeroed, 3)

            def power(rv, mv, eps_done, k, done):
                apart(pool)
                ts(rv, mv, EPS, None, ALU.add).then_inc(eps_done, 1)
                pool.wait_ge(eps_done, k + 1)
                tt(rv, rv, negh[:, 0:rv.shape[1]], ALU.pow).then_inc(done, 1)

            for i in range(2):
                last = pool.memset(BAND[i][:, :, :], 0.0)
            last.then_inc(zeroed, 1)
            for k in range(2):
                pool.wait_ge(f_mv, k + 1)
                power(RVa[:, :], MVa[:, :, 1], f_eps, k, f_rv)

            def step(n, odd, a, b, c, d):
                m, q = n - 1, n - 3
                if d:
                    pool.wait_ge(yc_ready, q + 1)
                    apart(pool)
                    ts(XS[:, :, 0:D // 2], YC[:, :, 0:D // 2], 0.0, None, ALU.add).then_inc(xs_lo, 1)
                    pool.wait_ge(small_in, 16 * 4)
                    pool.wait_ge(y_ready, NB + q)
                    tt(YCB[:, :, :], YC[:, :, :], wide(B2[:, one(layer(q)), :], 1, TILES),
                       ALU.add).then_inc(ycb_ready, 1)
                if a:
                    add(n, 0, 0, odd)
                    add(n, 0, 1, odd)
                if b:
                    norm(m, 0)
                if d:
                    pool.wait_ge(mv_done, q + 1)
                    power(RV[:, :], MV[:, :, 1], var_eps, q, rv_done)
                if a:
                    add(n, 0, 2, odd)
                    add(n, 0, 3, odd)
                if b:
                    norm(m, 1)
                if a:
                    for c in range(4):
                        add(n, 1, c, odd)

            def norm(m, t):
                pool.wait_ge(p_rsum, 2 * m + t + 1)
                tt(PB[:, t, :, :], PB[:, t, :, :],
                   wide(RS[:, t, :].rearrange("p (h a) -> p h a", a=1), 2, 2 * WIN), ALU.mult).then_inc(p_ready, 1)

            def add(n, t, c, odd):
                u, half = 2 * n + t, c % 2
                heads = slice(half * HPC, (half + 1) * HPC)
                cols = slice(half * CH, (half + 1) * CH)
                r = RK[:, heads] if c >= 2 else RQ[:, odd, t, heads]
                pool.wait_ge(sq_summed, 4 * u + c + 1)
                apart(pool)
                ts(r, SSQ[:, t, c // 2, heads], 1e-24, None, ALU.max).then_inc(ss_clamped, 1)
                pool.wait_ge(ss_clamped, 4 * u + c + 1)
                tt(r, r, negh[:, 0:HPC], ALU.pow).then_inc((rq_ready, rk_ready)[c // 2], 1)
                v = T1[:, t, c // 2, cols]
                if c < 2:
                    tt(v, v, T2q[:, t, cols], ALU.add).then_inc(q_ready, 1)
                else:
                    tt(v, v, T2k[:, cols], ALU.add).then_inc(k_added, 1)
                    pool.wait_ge(rk_ready, 2 * u + half + 1)
                    pool.wait_ge(k_added, 2 * u + half + 1)
                    v = v.rearrange("p (k d) -> p k d", k=HPC)
                    tt(v, v, wide(r.rearrange("p (h a) -> p h a", a=1), 2, DH), ALU.mult).then_inc(k_ready, 1)

            pipeline(pool, step, NBL, 3)


_INS = ['x', 'ctx_1024', 'g_xattn', 'g_ffn', 'L0_ffn_Wqkv', 'L0_ffn_q_scale', 'L0_ffn_k_scale', 'L0_ffn_Wo',
        'L0_ffn_ln_g', 'L0_ffn_ln_b', 'L0_ffn_W1', 'L0_ffn_b1', 'L0_ffn_W2', 'L0_ffn_b2']


def constants():
    import numpy as np
    f = np.float32
    half = np.arange(0, DH, 2, dtype=f)
    inv_freq = (f(1.0) / f(10000.0) ** (half / f(DH))).astype(f)
    t = np.arange(SEQ, dtype=f)
    freqs = (t[:, None] * inv_freq[None, :]).astype(f)
    base = ((half + f(0.4 * DH)) / f(1.4 * DH)).astype(f)
    power = ((t - SEQ // 2) / f(WIN // 2)).astype(f)
    scale = (base[None, :] ** power[:, None]).astype(f)
    cos, sin = np.cos(freqs).astype(f), np.sin(freqs).astype(f)
    both = np.stack([scale, f(1.0) / scale], 1)
    cs = (cos[:, None, :] * both).astype(f)
    sn = (sin[:, None, :] * both).astype(f)
    cs = np.concatenate([cs, cs], -1)
    sn = np.concatenate([-sn, sn], -1)
    cs[:, 0] *= f(QK_SCALE)
    sn[:, 0] *= f(QK_SCALE)

    def lay(v):
        return np.ascontiguousarray(v.reshape(TILES, P, -1).transpose(1, 0, 2).reshape(P, -1))

    i, j = np.arange(WIN)[:, None], np.arange(2 * WIN)[None, :]
    seen = (i <= j) & (j <= i + WIN)
    m = np.where(seen, f(0), f(-1e30)).astype(f)
    m = np.tile(m, (SEQ // WIN, 1)).reshape(SEQ // WIN, WIN, 2 * WIN)
    m[0, :, 0:WIN] = -1e30
    return {
        'c_cos': lay(cs), 'c_sin': lay(sn), 'c_mask': lay(m.reshape(SEQ, 2 * WIN)),
        'c_ident': np.eye(P, dtype=f), 'c_shift': np.eye(P, k=1, dtype=f),
        'c_carry': (np.arange(P)[:, None] == P - 1).astype(f) * (np.arange(P)[None, :] == 0).astype(f),
    }


def arrays_of(inputs):
    import numpy as np
    a = {name: np.ascontiguousarray(inputs[name]) for name in _INS}
    for name in ('L0_ffn_ln_g', 'L0_ffn_ln_b'):
        a[name] = np.ascontiguousarray(a[name].T)
    b1 = np.zeros((P, DEPTH, 2, len(FC)), a['L0_ffn_b1'].dtype)
    for half in range(2):
        for c, (f0, fn) in enumerate(FC):
            b1[0:fn, :, half, c] = a['L0_ffn_b1'][:, half * FF + f0:half * FF + f0 + fn].T
    a['L0_ffn_b1'] = b1.reshape(P, -1)
    return a | constants()


def kernel(**inputs):
    import concourse.bacc as bacc
    from concourse.bass_utils import run_bass_kernel_spmd

    nc = bacc.Bacc("TRN2", target_bir_lowering=False, num_devices=1)
    arrays = arrays_of(inputs)
    args = [nc.dram_tensor(f"in_{k}", a.shape, mybir.dt.from_np(a.dtype), kind="ExternalInput").ap()
            for k, a in arrays.items()]
    args.append(nc.dram_tensor("out", (NB, SEQ, D), F32, kind="ExternalOutput").ap())
    flamingo_kernel(nc, *args)
    r = run_bass_kernel_spmd(nc, [{f"in_{k}": a for k, a in arrays.items()}], core_ids=[0])
    return r.results[0]["out"]
```

```python
from contextlib import ExitStack

import concourse.bass as bass
from concourse import mybir

F32 = mybir.dt.float32
ALU = mybir.AluOpType
ACT = mybir.ActivationFunctionType
AX_X = mybir.AxisListType.X

P = 128
NB = 8
SEQ = 256
TILES = SEQ // P
D = 128
DEPTH = 6
HEADS = 16
DH = 64
HALF = DH // 2
WIN = 32
NWT = P // WIN
INNER = HEADS * DH
BLK = INNER // P
FF = int(D * 4 * 2 / 3)
FC = [(0, 128), (128, 128), (256, FF - 256)]
CH = 512
HPC = CH // DH
NBL = NB * DEPTH
EPS = 1e-5
QK_SCALE = 8.0
BANDW = P + WIN
CHUNKS = [(0, 0), (0, 1), (0, 2), (0, 3), (0, 4), (0, 5), (1, 4), (1, 5), (1, 0), (1, 1), (1, 2), (1, 3)]
PARTS = [(0, 12), (12, 16)]


def flamingo_kernel(nc, x, ctx, g_xattn, g_ffn, wqkv, q_scale, k_scale, wo, ln_g, ln_b, w1, b1, w2, b2,
                    c_cos, c_sin, c_mask, c_ident, c_shift, c_carry, out):
    x_v = x.rearrange("b (t p) d -> p (b t) d", p=P)
    ctx_v = ctx.rearrange("b (t p) d -> p (b t) d", p=P)
    out_v = out.rearrange("b (t p) d -> p (b t) d", p=P)

    with ExitStack() as es:
        def sb(name, shape):
            return es.enter_context(nc.sbuf_tensor(name, shape, F32))

        def bank(name, shape):
            return es.enter_context(nc.psum_tensor(name, shape, F32))

        def sem(name):
            return es.enter_context(nc.semaphore(name))

        Wqkv = sb("Wqkv", [P, 2, 3 * INNER])
        Wo = sb("Wo", [P, 2, BLK, D])
        W1 = sb("W1", [P, DEPTH, 2 * FF])
        W1c = sb("W1c", [P, 2 * FF])
        W2 = sb("W2", [P, DEPTH, len(FC), D])
        B1 = sb("B1", [P, DEPTH, 2, len(FC)])
        B2 = sb("B2", [P, DEPTH, D])
        G = sb("G", [P, DEPTH])
        Bt = sb("Bt", [P, DEPTH])
        TA = sb("TA", [P, DEPTH, TILES * 2 * DH])
        TB = sb("TB", [P, DEPTH, TILES * 2 * DH])
        cosc = sb("cosc", [P, TILES * 2 * DH])
        sinc = sb("sinc", [P, TILES * 2 * DH])
        mask = sb("mask", [P, TILES, 2 * WIN])
        ident = sb("ident", [P, P])
        shift = sb("shift", [P, P])
        carry = sb("carry", [P, P])
        negh = sb("negh", [P, HEADS])
        gates = sb("gates", [P, 2])
        tg = sb("tg", [P, 2])
        X1 = sb("X1", [P, NB * TILES, D])
        Y = sb("Y", [P, NB * TILES, D])
        YA = sb("YA", [P, TILES, D])
        YT = sb("YT", [P, SEQ])
        SQ = sb("SQ", [P, 2, CH])
        SSQ = sb("SSQ", [P, TILES, 2, HEADS])
        RK = sb("RK", [P, HEADS])
        RQ = sb("RQ", [P, 2, TILES, HEADS])
        T1 = sb("T1", [P, TILES, 2, INNER])
        T2q = sb("T2q", [P, TILES, INNER])
        T2k = sb("T2k", [P, INNER])
        QT = sb("QT", [P, BLK, SEQ])
        KT = sb("KT", [P, BLK, WIN + SEQ])
        V = sb("V", [P, 2, TILES, INNER])
        PB = sb("PB", [P, TILES, HEADS, 2 * WIN])
        NMX = sb("NMX", [P, TILES, HEADS])
        SS = sb("SS", [P, TILES, HEADS])
        RS = sb("RS", [P, TILES, HEADS])
        BAND = [sb("BAND0", [P, HEADS, BANDW]), sb("BAND1", [P, HEADS, P])]
        OTS = sb("OTS", [P, BLK, SEQ])
        YC = sb("YC", [P, TILES, D])
        YCB = sb("YCB", [P, TILES, D])
        XS = sb("XS", [P, TILES, D])
        XN = sb("XN", [P, TILES, D])
        XNT = sb("XNT", [P, SEQ])
        BS = sb("BS", [P, TILES, 6])
        MV = sb("MV", [P, TILES, 2])
        RV = sb("RV", [P, TILES])
        BSa = sb("BSa", [P, NB * TILES, 6])
        MVa = sb("MVa", [P, NB * TILES, 2])
        RVa = sb("RVa", [P, NB * TILES])
        G1 = sb("G1", [P, 2, SEQ])
        U = sb("U", [P, len(FC), SEQ])
        CTX = T2q[:, :, :].rearrange("p a n -> p (a n)").rearrange("p (k d) -> p k d", d=D)
        QS = QT[:, 0:3, :].rearrange("p a n -> p (a n)").rearrange("p (l n) -> p l n", l=DEPTH)
        XNs = [XN, XS]
        CTs = [YC, YCB]
        XCT = [OTS[:, 2 * i:2 * i + 2, :].rearrange("p a n -> p (a n)") for i in range(2)]
        Us = [OTS[:, 4 + 2 * i:6 + 2 * i, :].rearrange("p a n -> p (a n)") for i in range(2)]
        Gs = [PB[:, i, 0:HPC, :].rearrange("p h n -> p (h n)") for i in range(2)]

        KB = [bank(f"KB{i}", [P, CH]) for i in range(2)]
        TQ = [bank(f"TQ{i}", [P, CH]) for i in range(2)]
        SP = [bank(f"SP{i}", [P, BLK, 2 * WIN]) for i in range(2)]
        FP = [sp[:, :, :].rearrange("p k n -> p (k n)") for sp in SP]
        M0 = bank("M0", [P, CH])
        M1 = bank("M1", [P, CH])
        HB = [M1, M0, M1]
        M0t = M0[:, 0:TILES * D].rearrange("p (t d) -> p t d", t=TILES)

        x_in = sem("x_in")
        ctx_in = sem("ctx_in")
        const_in = sem("const_in")
        scale_in = sem("scale_in")
        small_in = sem("small_in")
        ffn_in = sem("ffn_in")
        wqkv_in = sem("wqkv_in")
        wo_in = sem("wo_in")
        zeroed = sem("zeroed")
        tanh_done = sem("tanh_done")
        tab_done = sem("tab_done")
        f_stats = sem("f_stats")
        f_mv = sem("f_mv")
        f_eps = sem("f_eps")
        f_rv = sem("f_rv")
        f_xn = sem("f_xn")
        f_cts = sem("f_cts")
        f_tr = sem("f_tr")
        f_ev = sem("f_ev")
        f_h = sem("f_h")
        f_gelu = sem("f_gelu")
        f_u = sem("f_u")
        f_o = sem("f_o")
        f_x1 = sem("f_x1")
        ya_copied = sem("ya_copied")
        xt_mm = sem("xt_mm")
        yt_ready = sem("yt_ready")
        chunk_mm = sem("chunk_mm")
        v_evac = sem("v_evac")
        sq_done = sem("sq_done")
        rope_done = sem("rope_done")
        sq_summed = sem("sq_summed")
        k_added = sem("k_added")
        ss_clamped = sem("ss_clamped")
        rq_ready = sem("rq_ready")
        rk_ready = sem("rk_ready")
        q_ready = sem("q_ready")
        k_ready = sem("k_ready")
        tq_mm = sem("tq_mm")
        tq_evac = sem("tq_evac")
        ot_mm = sem("ot_mm")
        ot_evac = sem("ot_evac")
        sims_mm = sem("sims_mm")
        s_masked = sem("s_masked")
        s_max = sem("s_max")
        s_shifted = sem("s_shifted")
        p_exp = sem("p_exp")
        p_rsum = sem("p_rsum")
        p_ready = sem("p_ready")
        band_ready = sem("band_ready")
        pj_mm = sem("pj_mm")
        yc_ready = sem("yc_ready")
        fx_mm = sem("fx_mm")
        xs_hi = sem("xs_hi")
        xs_lo = sem("xs_lo")
        ycb_ready = sem("ycb_ready")
        bn_done = sem("bn_done")
        mv_done = sem("mv_done")
        var_eps = sem("var_eps")
        rv_done = sem("rv_done")
        xn_ready = sem("xn_ready")
        ft_mm = sem("ft_mm")
        xnt_ready = sem("xnt_ready")
        w1c_ready = sem("w1c_ready")
        h_mm = sem("h_mm")
        g_ready = sem("g_ready")
        u_done = sem("u_done")
        po_mm = sem("po_mm")
        y_ready = sem("y_ready")
        o_ready = sem("o_ready")
        out_done = sem("out_done")
        waited = sem("waited")

        def wide(ap, dim, n):
            shape = list(ap.shape)
            shape[dim] = n
            return ap.broadcast_to(shape)

        def batch(n):
            return bass.ds((n & (NB - 1)) * TILES, TILES)

        def layer(n):
            if isinstance(n, int):
                return n // NB
            return nc.s_assert_within(n // NB, 0, DEPTH - 1,
                                      skip_runtime_bounds_check_because="steps end before NBL = NB * DEPTH")

        def one(i):
            return bass.ds(i, 1)

        def after(eng, s, count):
            if not isinstance(count, int) or count > 0:
                eng.wait_ge(s, count)

        def apart(eng):
            eng.sem_inc(waited, 1)

        def pipeline(eng, step, steps, depth):
            def at(n):
                return [0 <= n - k < steps for k in range(depth + 1)]

            first = depth + depth % 2
            for n in range(first):
                step(n, n % 2, *at(n))
            with eng.Fori(first, steps, 2) as i:
                step(i, 0, *[True] * (depth + 1))
                step(i + 1, 1, *[True] * (depth + 1))
            for n in range(steps, steps + depth):
                step(n, n % 2, *at(n))

        def units(n, *on):
            return [n - k if there else None for k, there in enumerate(on)]

        block = es.enter_context(nc.Block())

        @block.sync
        def _(sp):
            sp.dma_start(X1[:, :, :], x_v).then_inc(x_in, 16)
            sp.dma_start(CTX, ctx_v).then_inc(ctx_in, 16)
            for l in range(DEPTH):
                sp.dma_start(QS[:, l, 0:DH], wide(q_scale[l:l + 1, :], 0, P)).then_inc(scale_in, 16)
                sp.dma_start(QS[:, l, DH:2 * DH], wide(k_scale[l:l + 1, :], 0, P)).then_inc(scale_in, 16)
            sp.dma_start(ident[:, :], c_ident).then_inc(const_in, 16)
            sp.dma_start(shift[:, :], c_shift).then_inc(const_in, 16)
            sp.dma_start(carry[:, :], c_carry).then_inc(const_in, 16)
            sp.dma_start(cosc[:, :], c_cos).then_inc(const_in, 16)
            sp.dma_start(sinc[:, :], c_sin).then_inc(const_in, 16)
            sp.dma_start(mask[:, :, :].rearrange("p t n -> p (t n)"), c_mask).then_inc(const_in, 16)
            sp.dma_start(gates[:, 0:1], wide(g_xattn.rearrange("(a n) -> a n", a=1), 0, P)).then_inc(const_in, 16)
            sp.dma_start(gates[:, 1:2], wide(g_ffn.rearrange("(a n) -> a n", a=1), 0, P)).then_inc(const_in, 16)
            sp.dma_start(W1[:, :, :], w1.rearrange("l d n -> d l n")).then_inc(ffn_in, 16)
            for c, (f0, fn) in enumerate(FC):
                sp.dma_start(W2[0:fn, :, c, :], w2[:, f0:f0 + fn, :].rearrange("l f d -> f l d")).then_inc(ffn_in, 16)
            sp.dma_start(B2[:, :, :], wide(b2.rearrange("(a l) d -> a l d", a=1), 0, P)).then_inc(small_in, 16)
            sp.dma_start(G[:, :], ln_g).then_inc(small_in, 16)
            sp.dma_start(Bt[:, :], ln_b).then_inc(small_in, 16)
            sp.dma_start(B1[:, :, :, :].rearrange("p l h c -> p (l h c)"), b1).then_inc(small_in, 16)

            def load_layer(l, slot):
                sp.dma_start(Wqkv[:, one(slot), :].rearrange("p a n -> p (a n)"),
                             wqkv[one(l), :, :].rearrange("a d n -> (a d) n")).then_inc(wqkv_in, 16)
                sp.dma_start(Wo[:, one(slot), :, :].rearrange("p a k d -> p (a k) d"),
                             wo[one(l), :, :].rearrange("a (k p) d -> p (a k) d", p=P)).then_inc(wo_in, 16)

            load_layer(0, 0)
            sp.wait_ge(wqkv_in, 16)
            sp.wait_ge(wo_in, 16)
            load_layer(1, 1)
            with sp.Fori(2, DEPTH, 1) as l:
                sp.wait_ge(wqkv_in, 16 * l)
                sp.wait_ge(wo_in, 16 * l)
                sp.wait_ge(pj_mm, (l - 1) * NB)
                apart(sp)
                load_layer(l, l & 1)
            for i, (t0, t1) in enumerate(PARTS):
                sp.wait_ge(o_ready, i + 1)
                sp.dma_start(out_v[:, t0:t1, :], Y[:, t0:t1, :]).then_inc(out_done, 16)
            sp.wait_ge(out_done, 16 * len(PARTS))

        @block.tensor
        def _(pe):
            mm, tr = pe.matmul, pe.transpose

            def first(n, odd, a, b, c):
                if b:
                    pe.wait_ge(f_ev, n)
                    after(pe, f_u, n - 2)
                    xct = XCT[1 - odd]
                    for f in range(TILES):
                        last = mm(FP[1 - odd][:, f * SEQ:(f + 1) * SEQ], xct[:, SEQ + f * P:SEQ + (f + 1) * P],
                                  xct[:, 0:SEQ], start=True, stop=True)
                    last.then_inc(f_h, 1)
                if c:
                    pe.wait_ge(f_u, n - 1)
                    after(pe, f_x1, n - 2)
                    for t in range(TILES):
                        for f in range(TILES):
                            last = mm(KB[odd][:, t * D:(t + 1) * D],
                                      Us[odd][:, f * SEQ + t * P:f * SEQ + (t + 1) * P], CTs[odd][:, f, :],
                                      start=(f == 0), stop=(f == TILES - 1))
                    last.then_inc(f_o, 1)
                if a:
                    pe.wait_ge(f_xn, n + 1)
                    pe.wait_ge(f_cts, n + 1)
                    after(pe, f_ev, n - 1)
                    for t in range(TILES):
                        tr(TQ[odd][:, t * P:(t + 1) * P], XNs[odd][:, t, :], ident[:, :])
                        last = tr(TQ[odd][:, SEQ + t * P:SEQ + (t + 1) * P], CTs[odd][:, t, :], ident[:, :])
                    last.then_inc(f_tr, 1)

            pe.wait_ge(const_in, 16 * 8)
            pipeline(pe, first, NB, 2)
            pe.wait_ge(f_x1, NB)

            def step(n, odd, a, b, c, d):
                u0, u1, u2, u3 = units(n, a, b, c, d)
                turn_y(u0, d)
                turn(u1, 0, 0)
                turn(u1, 0, 1)
                shifted(u3, a)
                qkv(u0, 0)
                turn(u1, 0, 2)
                turn(u1, 0, 3)
                qkv(u0, 1)
                sims(u1, 0, 0)
                sims(u1, 0, 1)
                turn(u1, 1, 0)
                qkv(u0, 2)
                turn_xn(u3)
                turn(u1, 1, 1)
                qkv(u0, 3)
                turn(u1, 1, 2)
                turn(u1, 1, 3)
                ffn_in_mm(u3, 0)
                sims(u1, 1, 0)
                ffn_in_mm(u3, 1)
                sims(u1, 1, 1)
                qkv(u0, 4)
                attend(u2, odd, b, 0)
                attend(u2, odd, b, 1)
                attend(u2, odd, b, 2)
                attend(u2, odd, b, 3)
                qkv(u0, 5)
                qkv(u0, 6)
                qkv(u0, 7)
                ffn_in_mm(u3, 2)
                qkv(u0, 8)
                qkv(u0, 9)
                project(u2, d)
                qkv(u0, 10)
                qkv(u0, 11)
                ffn_out_mm(u3, c)

            def turn_y(n, d):
                if n is None:
                    return
                pe.wait_ge(ya_copied, n + 1)
                if d:
                    after(pe, u_done, 3 * (n - 3))
                for t in range(TILES):
                    last = tr(M1[:, t * P:(t + 1) * P], YA[:, t, :], ident[:, :])
                last.then_inc(xt_mm, 1)

            def shifted(q, a):
                if q is None:
                    return
                if a:
                    pe.wait_ge(yt_ready, q + 4)
                else:
                    pe.wait_ge(u_done, 3 * q)
                pe.wait_ge(yc_ready, q + 1)
                fx = M1[:, 0:TILES * HALF * 2].rearrange("p (t d) -> p t d", t=TILES)
                mm(fx, shift[:, :], YC[:, :, D // 2:D], start=True, stop=False, skip_group_check=True)
                mm(fx[:, 1, :], carry[:, :], YC[:, 0, D // 2:D], start=False, stop=True,
                   skip_group_check=True).then_inc(fx_mm, 1)

            def turn_xn(q):
                if q is None:
                    return
                pe.wait_ge(xn_ready, q + 1)
                for t in range(TILES):
                    last = tr(M1[:, t * P:(t + 1) * P], XN[:, t, :], ident[:, :])
                last.then_inc(ft_mm, 1)

            def qkv(n, i):
                if n is None:
                    return
                t, c = CHUNKS[i]
                if i == 0:
                    pe.wait_ge(yt_ready, n + 1)
                    pe.wait_ge(wqkv_in, 16 * (layer(n) + 1))
                if i < 2:
                    after(pe, rope_done, 8 * n - 1 + i)
                elif i < 6:
                    pe.wait_ge(rope_done, 8 * n + i - 1)
                elif i < 10:
                    pe.wait_ge(v_evac, 4 * n + i - 5)
                else:
                    pe.wait_ge(rope_done, 8 * n + i - 5)
                mm(KB[i % 2][:, :], YT[:, t * P:(t + 1) * P],
                   Wqkv[:, one(layer(n) & 1), c * CH:(c + 1) * CH].rearrange("p a n -> p (a n)"),
                   start=True, stop=True).then_inc(chunk_mm, 1)

            def turn(m, t, g):
                if m is None:
                    return
                pe.wait_ge((q_ready, k_ready)[g // 2], 4 * m + 2 * t + g % 2 + 1)
                if t == 0 and g < 2:
                    after(pe, ot_evac, 4 * (m - 2) + 3 + g)
                else:
                    pe.wait_ge(tq_evac, 8 * m + 4 * t + g - 1)
                for k in range(4):
                    c = (g % 2) * CH + k * P
                    last = tr(TQ[g % 2][:, k * P:(k + 1) * P], T1[:, t, g // 2, c:c + P], ident[:, :])
                last.then_inc(tq_mm, 1)

            def sims(m, t, half):
                if m is None:
                    return
                if half == 0:
                    pe.wait_ge(tq_evac, 8 * m + 4 * t + 4)
                    after(pe, s_masked, 2 * m + t)
                    apart(pe)
                for blk in range(half * BLK // 2, (half + 1) * BLK // 2):
                    for w in range(NWT):
                        for a in range(2):
                            rows = slice(DH * a, DH * a + DH)
                            c = t * P + w * WIN
                            last = mm(SP[a][WIN * w:WIN * w + WIN, blk, :], QT[rows, blk, c:c + WIN],
                                      KT[rows, blk, c:c + 2 * WIN], start=True, stop=True)
                if half:
                    last.then_inc(sims_mm, 1)

            def attend(m, odd, turned, k):
                if m is None:
                    return
                if k == 0:
                    pe.wait_ge(band_ready, m + 1)
                    pe.wait_ge(v_evac, 4 * m + 4)
                if k < 2 and turned:
                    pe.wait_ge(tq_evac, 8 * m + 15 + k)
                else:
                    pe.wait_ge(ot_evac, 4 * m + k - 1)
                for i in range(2):
                    blk = 2 * k + i
                    for a in range(2):
                        h = 2 * blk + a
                        o = TQ[k % 2][DH * a:DH * a + DH, i * SEQ:(i + 1) * SEQ]
                        mm(o[:, P:SEQ], V[:, odd, 1, h * DH:(h + 1) * DH], BAND[1][:, a * BLK + blk, :],
                           start=True, stop=False, skip_group_check=True)
                        last = mm(o[:, 0:BANDW], V[:, odd, 0, h * DH:(h + 1) * DH], BAND[0][:, a * BLK + blk, :],
                                  start=False, stop=True, skip_group_check=True)
                last.then_inc(ot_mm, 1)

            def project(m, d):
                if m is None:
                    return
                pe.wait_ge(ot_evac, 4 * m + 4)
                if d:
                    pe.wait_ge(u_done, 3 * m - 1)
                pe.wait_ge(wo_in, 16 * (layer(m) + 1))
                for t in range(TILES):
                    for blk in range(BLK):
                        last = mm(M0t[:, t, :], OTS[:, blk, t * P:(t + 1) * P],
                                  Wo[:, one(layer(m) & 1), blk, :].rearrange("p a d -> p (a d)"),
                                  start=(blk == 0), stop=(blk == BLK - 1))
                last.then_inc(pj_mm, 1)

            def ffn_in_mm(q, c):
                if q is None:
                    return
                f0, fn = FC[c]
                if c == 0:
                    pe.wait_ge(xnt_ready, q + 1)
                    pe.wait_ge(w1c_ready, q + 1)
                elif c == 1:
                    pe.wait_ge(y_ready, NB + q)
                else:
                    pe.wait_ge(u_done, 3 * q + 1)
                for half in range(2):
                    last = mm(HB[c][0:fn, half * SEQ:(half + 1) * SEQ],
                              W1c[:, half * FF + f0:half * FF + f0 + fn], XNT[:, :], start=True, stop=True)
                last.then_inc(h_mm, 1)

            def ffn_out_mm(q, c):
                if q is None:
                    return
                pe.wait_ge(u_done, 3 * q + 3)
                if c:
                    pe.wait_ge(yc_ready, q + 2)
                for t in range(TILES):
                    for k, (f0, fn) in enumerate(FC):
                        last = mm(M0t[:, t, :], U[0:fn, k, t * P:(t + 1) * P],
                                  W2[0:fn, one(layer(q)), k, :].rearrange("p a d -> p (a d)"),
                                  start=(k == 0), stop=(k == len(FC) - 1))
                last.then_inc(po_mm, 1)

            pipeline(pe, step, NBL, 3)

        @block.scalar
        def _(act):
            f = act.activation
            act.wait_ge(const_in, 16 * 8)
            f(tg[:, :], gates[:, :], ACT.Tanh).then_inc(tanh_done, 1)
            act.wait_ge(ctx_in, 16)

            def first(n, odd, a, b, c):
                if b:
                    act.wait_ge(f_h, n)
                    f(Gs[1 - odd], FP[1 - odd], ACT.Gelu).then_inc(f_gelu, 1)
                if a:
                    after(act, f_o, n - 1)
                    f(CTs[odd][:, :, :], CTX[:, batch(n), :], ACT.Copy).then_inc(f_cts, 1)
                    act.wait_ge(f_tr, n + 1)
                    f(XCT[odd], TQ[odd][:, :], ACT.Copy).then_inc(f_ev, 1)

            pipeline(act, first, NB, 2)

            def step(n, odd, a, b, c, d):
                u0, u1, u2, u3 = units(n, a, b, c, d)
                copy_y(u0)
                square(u1, 1, 3)
                evac_y(u0)
                evac_turned(u1, 0, 0)
                evac_turned(u1, 0, 1)
                high_half(u3)
                low_half(u3)
                square(u0, 0, 0)
                evac_turned(u1, 0, 2)
                evac_turned(u1, 0, 3)
                square(u0, 0, 1)
                exps(u2, 1, odd, 1)
                evac_turned(u1, 1, 0)
                evac_xn(u3)
                square(u0, 0, 2)
                evac_turned(u1, 1, 1)
                square(u0, 0, 3)
                evac_turned(u1, 1, 2)
                evac_turned(u1, 1, 3)
                exps(u1, 0, 1 - odd, 0)
                exps(u1, 0, 1 - odd, 1)
                evac_o(u2, 0)
                evac_o(u2, 1)
                gelu(u3, 0)
                evac_v(u0, 0, odd, 0)
                evac_v(u0, 0, odd, 1)
                evac_o(u2, 2)
                gelu(u3, 1)
                evac_v(u0, 1, odd, 0)
                evac_o(u2, 3)
                evac_v(u0, 1, odd, 1)
                copy_w1(u2)
                square(u0, 1, 0)
                gelu(u3, 2)
                square(u0, 1, 1)
                exps(u1, 1, 1 - odd, 0)
                square(u0, 1, 2)

            def copy_y(n):
                if n is None:
                    return
                act.wait_ge(y_ready, n + 1)
                after(act, xt_mm, n)
                f(YA[:, :, :], Y[:, batch(n), :], ACT.Copy).then_inc(ya_copied, 1)

            def evac_y(n):
                if n is None:
                    return
                act.wait_ge(xt_mm, n + 1)
                f(YT[0:D // 2, :], M1[0:D // 2, 0:SEQ], ACT.Copy)
                f(YT[D // 2:D, 1:SEQ], M1[D // 2:D, 0:SEQ - 1], ACT.Copy).then_inc(yt_ready, 1)

            def low_half(q):
                if q is None:
                    return
                act.wait_ge(yc_ready, q + 1)
                f(XS[:, :, 0:D // 2], YC[:, :, 0:D // 2], ACT.Copy).then_inc(xs_lo, 1)

            def high_half(q):
                if q is None:
                    return
                act.wait_ge(fx_mm, q + 1)
                f(XS[:, :, D // 2:D], M1[:, 0:TILES * D // 2].rearrange("p (t d) -> p t d", t=TILES),
                  ACT.Copy).then_inc(xs_hi, 1)

            def copy_w1(q):
                if q is None:
                    return
                after(act, h_mm, 3 * q)
                act.wait_ge(ffn_in, 16 * 4)
                f(W1c[:, :], W1[:, one(layer(q)), :].rearrange("p a n -> p (a n)"), ACT.Copy).then_inc(w1c_ready, 1)

            def evac_xn(q):
                if q is None:
                    return
                act.wait_ge(ft_mm, q + 1)
                act.wait_ge(small_in, 16 * 4)
                f(XNT[:, :], M1[:, 0:SEQ], ACT.Identity, bias=Bt[:, one(layer(q))],
                  scale=G[:, one(layer(q))]).then_inc(xnt_ready, 1)

            def gelu(q, k):
                if q is None:
                    return
                fn = FC[k][1]
                act.wait_ge(h_mm, 3 * q + k + 1)
                f(G1[0:fn, k % 2, :], HB[k][0:fn, SEQ:2 * SEQ], ACT.Gelu,
                  bias=B1[0:fn, one(layer(q)), 1, k]).then_inc(g_ready, 1)

            def evac_o(m, k):
                if m is None:
                    return
                act.wait_ge(ot_mm, 4 * m + k + 1)
                f(OTS[:, 2 * k:2 * k + 2, :], TQ[k % 2][:, :].rearrange("p (k n) -> p k n", k=2),
                  ACT.Copy).then_inc(ot_evac, 1)

            def evac_turned(m, t, g):
                if m is None:
                    return
                act.wait_ge(tq_mm, 8 * m + 4 * t + g + 1)
                to, c0 = (QT, t * P) if g < 2 else (KT, WIN + t * P)
                f(to[:, 4 * (g % 2):4 * (g % 2) + 4, c0:c0 + P],
                  TQ[g % 2][:, :].rearrange("p (k n) -> p k n", k=4), ACT.Copy).then_inc(tq_evac, 1)

            def exps(m, t, odd, a):
                if m is None:
                    return
                act.wait_ge(s_shifted, 2 * m + t + 1)
                for blk in range(BLK):
                    i, h = a * BLK + blk, 2 * blk + a
                    last = f(PB[:, t, i, :], PB[:, t, i, :], ACT.Exp, bias=NMX[:, t, i:i + 1],
                             scale=RQ[:, odd, t, h:h + 1], accum_out=SS[:, t, i:i + 1])
                if a:
                    last.then_inc(p_exp, 1)

            def evac_v(n, t, odd, j):
                if n is None:
                    return
                if t == 0 and j == 0:
                    after(act, ot_mm, 4 * (n - 1))
                act.wait_ge(chunk_mm, 12 * n + CHUNKS.index((t, 4 + j)) + 1)
                f(V[:, odd, t, j * CH:(j + 1) * CH], KB[j][:, :], ACT.Copy).then_inc(v_evac, 1)

            def square(n, t, c):
                if n is None:
                    return
                act.wait_ge(chunk_mm, 12 * n + CHUNKS.index((t, c)) + 1)
                after(act, sq_summed, 8 * n + 4 * t + c - 1)
                f(SQ[:, c % 2, :], KB[c % 2][:, :], ACT.Square).then_inc(sq_done, 1)

            pipeline(act, step, NBL, 3)

        @block.vector
        def _(dve):
            tt, ts, stt = dve.tensor_tensor, dve.tensor_scalar, dve.scalar_tensor_tensor
            dve.memset(YT[D // 2:D, 0:1], 0.0).then_inc(zeroed, 1)
            dve.memset(KT[:, :, 0:WIN], 0.0).then_inc(zeroed, 1)

            def batch_stats(n):
                for t in range(TILES):
                    i = (n & (NB - 1)) * TILES + t
                    last = dve.bn_stats(BSa[:, one(i), :].rearrange("p a n -> p (a n)"),
                                        X1[:, one(i), :].rearrange("p a n -> p (a n)"))
                last.then_inc(f_stats, 1)

            def means(k):
                dve.wait_ge(f_stats, (k + 1) * NB)
                for i in range(NB * TILES):
                    last = dve.bn_aggr(MVa[:, i, :], BSa[:, i, :])
                last.then_inc(f_mv, 1)

            def normalize(to, i):
                return ts(to, X1[:, one(i), :].rearrange("p a d -> p (a d)"), MVa[:, one(i), 0], RVa[:, one(i)],
                          ALU.subtract, ALU.mult)

            def first(n, odd, a, b, c):
                if a:
                    after(dve, f_tr, n - 1)
                    for t in range(TILES):
                        last = normalize(XNs[odd][:, t, :], (n & (NB - 1)) * TILES + t)
                    last.then_inc(f_xn, 1)
                if b:
                    dve.wait_ge(f_gelu, n)
                    after(dve, f_o, n - 2)
                    tt(Us[1 - odd], FP[1 - odd], Gs[1 - odd], ALU.mult).then_inc(f_u, 1)
                if c:
                    dve.wait_ge(f_o, n - 1)
                    stt(out=X1[:, batch(n - 2), :], in0=KB[odd][:, 0:TILES * D].rearrange("p (t d) -> p t d", t=TILES),
                        scalar=tg[:, 0:1], in1=X1[:, batch(n - 2), :], op0=ALU.mult, op1=ALU.add).then_inc(f_x1, 1)
                    dve.wait_ge(f_x1, n - 1)
                    apart(dve)
                    batch_stats(n - 2)

            dve.wait_ge(x_in, 16)
            for n in range(NB):
                batch_stats(n)
            means(0)

            dve.wait_ge(scale_in, 16 * 2 * DEPTH)
            dve.wait_ge(const_in, 16 * 8)
            qs = QS[:, :, :].rearrange("p l (c s d) -> p l c s d", c=2, s=2)
            for l in range(DEPTH):
                for t in range(TILES):
                    cols = slice(t * 2 * DH, (t + 1) * 2 * DH)
                    tt(TA[:, l, cols], cosc[:, cols], QS[:, l, :], ALU.mult)
                    last = tt(TB[:, l, cols].rearrange("p (c s d) -> p c s d", c=2, s=2),
                              sinc[:, cols].rearrange("p (c s d) -> p c s d", c=2, s=2),
                              qs[:, l, :, ::-1, :], ALU.mult)
            last.then_inc(tab_done, 1)

            dve.wait_ge(f_rv, 1)
            dve.wait_ge(tanh_done, 1)
            pipeline(dve, first, NB, 2)
            means(1)
            dve.wait_ge(f_rv, 2)
            for i in range(NB * TILES):
                last = normalize(Y[:, i, :], i)
                if i % TILES == TILES - 1:
                    last.then_inc(y_ready, 1)
            dve.wait_ge(tab_done, 1)

            def step(n, odd, a, b, c, d):
                u0, u1, u2, u3 = units(n, a, b, c, d)
                rope(u1, 1, 3)
                stats(u3)
                rope(u0, 0, 0)
                rope(u0, 0, 1)
                normalize_xs(u3)
                masked(u1, 0)
                inverse_sums(u2, 1)
                shifts(u1, 0, 1 - odd)
                rope(u0, 0, 2)
                bands(u2, 1)
                masked(u1, 1)
                inverse_sums(u1, 0)
                shifts(u1, 1, 1 - odd)
                rope(u0, 0, 3)
                gated(u3, 0)
                bands(u1, 0)
                gated(u3, 1)
                rope(u0, 1, 0)
                add_b2(u3)
                rope(u0, 1, 1)
                gated(u3, 2)
                add_heads(u2)
                rope(u0, 1, 2)
                add_ffn(u3)
                if not a and n - 2 < NBL <= n - 1:
                    finish(0)

            def stats(q):
                if q is None:
                    return
                dve.wait_ge(xs_hi, q + 1)
                dve.wait_ge(xs_lo, q + 1)
                apart(dve)
                for t in range(TILES):
                    last = dve.bn_stats(BS[:, t, :], XS[:, t, :])
                last.then_inc(bn_done, 1)
                dve.wait_ge(bn_done, q + 1)
                apart(dve)
                for t in range(TILES):
                    last = dve.bn_aggr(MV[:, t, :], BS[:, t, :])
                last.then_inc(mv_done, 1)

            def normalize_xs(q):
                if q is None:
                    return
                dve.wait_ge(rv_done, q + 1)
                for t in range(TILES):
                    last = ts(XN[:, t, :], XS[:, t, :], MV[:, t, 0:1], RV[:, t:t + 1], ALU.subtract, ALU.mult)
                last.then_inc(xn_ready, 1)

            def gated(q, k):
                if q is None:
                    return
                fn = FC[k][1]
                dve.wait_ge(g_ready, 3 * q + k + 1)
                stt(out=U[0:fn, k, :], in0=HB[k][0:fn, 0:SEQ], scalar=B1[0:fn, one(layer(q)), 0, k],
                    in1=G1[0:fn, k % 2, :], op0=ALU.add, op1=ALU.mult).then_inc(u_done, 1)

            def add_heads(m):
                if m is None:
                    return
                dve.wait_ge(pj_mm, m + 1)
                after(dve, ycb_ready, m)
                tt(YC[:, :, :], M0t, Y[:, batch(m), :], ALU.add).then_inc(yc_ready, 1)

            def add_ffn(q):
                if q is None:
                    return
                dve.wait_ge(po_mm, q + 1)
                dve.wait_ge(ycb_ready, q + 1)
                tt(Y[:, batch(q), :], M0t, YCB[:, :, :], ALU.add).then_inc(y_ready, 1)

            def add_b2(q):
                if q is None:
                    return
                dve.wait_ge(small_in, 16 * 4)
                dve.wait_ge(yc_ready, q + 1)
                after(dve, y_ready, NB + q)
                tt(YCB[:, :, :], YC[:, :, :], wide(B2[:, one(layer(q)), :], 1, TILES), ALU.add).then_inc(ycb_ready, 1)

            def bands(m, t):
                if m is None:
                    return
                dve.wait_ge(p_ready, 2 * m + t + 1)
                if t == 0:
                    after(dve, ot_mm, 4 * m)
                    dve.wait_ge(zeroed, 4)
                else:
                    band(0, NWT - 1, 1, 0, 0, P)
                for v in range(NWT):
                    last = band(t, v, t, v, WIN, v * WIN)
                    if v < NWT - 1:
                        last = band(t, v, t, v + 1, 0, (v + 1) * WIN)
                if t:
                    last.then_inc(band_ready, 1)

            def finish(i):
                t0, t1 = PARTS[i]
                dve.wait_ge(y_ready, NBL + t1 // TILES)
                stt(out=Y[:, t0:t1, :], in0=Y[:, t0:t1, :], scalar=tg[:, 1:2], in1=X1[:, t0:t1, :],
                    op0=ALU.mult, op1=ALU.add).then_inc(o_ready, 1)

            def band(kt, v, pt, w, j, c):
                return dve.transpose(BAND[kt][WIN * v:WIN * v + WIN, :, c:c + WIN],
                                     PB[WIN * w:WIN * w + WIN, pt, :, j:j + WIN])

            def masked(m, t):
                if m is None:
                    return
                dve.wait_ge(sims_mm, 2 * m + t + 1)
                if t:
                    after(dve, band_ready, m)
                for a in range(2):
                    last = tt(PB[:, t, a * BLK:(a + 1) * BLK, :], SP[a][:, :, :],
                              wide(mask[:, t:t + 1, :], 1, BLK), ALU.add)
                last.then_inc(s_masked, 1)

            def shifts(m, t, odd):
                if m is None:
                    return
                dve.wait_ge(s_masked, 2 * m + t + 1)
                dve.tensor_reduce(NMX[:, t, :], PB[:, t, :, :], AX_X, ALU.max).then_inc(s_max, 1)
                dve.wait_ge(s_max, 2 * m + t + 1)
                dve.wait_ge(rq_ready, 4 * m + 2 * t + 2)
                nmx = NMX[:, t, :].rearrange("p (a k) -> p a k", a=2)
                stt(out=nmx, in0=nmx, scalar=-1.0, in1=RQ[:, odd, t, :].rearrange("p (k a) -> p a k", a=2),
                    op0=ALU.mult, op1=ALU.mult).then_inc(s_shifted, 1)

            def inverse_sums(m, t):
                if m is None:
                    return
                dve.wait_ge(p_exp, 2 * m + t + 1)
                dve.reciprocal(RS[:, t, :], SS[:, t, :]).then_inc(p_rsum, 1)

            def rope(n, t, c):
                if n is None:
                    return
                h = c // 2
                dve.wait_ge(sq_done, 8 * n + 4 * t + c + 1)
                if c < 2:
                    after(dve, q_ready, 4 * n + 2 * t - 3 + c)
                else:
                    after(dve, k_added, 4 * n + 2 * t - 3 + c)
                t2 = T2k[:, :] if h else T2q[:, t, :]
                raw = KB[c % 2][:, :]
                cols = slice((c % 2) * CH, (c % 2 + 1) * CH)
                tab = slice((t * 2 + h) * DH, (t * 2 + h + 1) * DH)
                tt(T1[:, t, h, cols].rearrange("p (k d) -> p k d", k=HPC), raw.rearrange("p (k d) -> p k d", k=HPC),
                   wide(TA[:, one(layer(n)), tab], 1, HPC), ALU.mult)
                last = tt(t2[:, cols].rearrange("p (k s d) -> p k s d", k=HPC, s=2),
                          raw.rearrange("p (k s d) -> p k s d", k=HPC, s=2)[:, :, ::-1, :],
                          wide(TB[:, one(layer(n)), tab].rearrange("p a (s d) -> p a s d", s=2), 1, HPC), ALU.mult)
                last.then_inc(rope_done, 1)
                dve.tensor_reduce(SSQ[:, t, h, (c % 2) * HPC:(c % 2 + 1) * HPC],
                                  SQ[:, c % 2, :].rearrange("p (k d) -> p k d", k=HPC), AX_X, ALU.add
                                  ).then_inc(sq_summed, 1)

            pipeline(dve, step, NBL, 3)
            finish(1)

        @block.gpsimd
        def _(pool):
            tt, ts = pool.tensor_tensor, pool.tensor_scalar
            pool.memset(negh[:, :], -0.5).then_inc(zeroed, 1)
            pool.wait_ge(zeroed, 3)

            def power(rv, mv, eps_done, k, done):
                apart(pool)
                ts(rv, mv, EPS, None, ALU.add).then_inc(eps_done, 1)
                pool.wait_ge(eps_done, k + 1)
                tt(rv, rv, negh[:, 0:rv.shape[1]], ALU.pow).then_inc(done, 1)

            for i in range(2):
                last = pool.memset(BAND[i][:, :, :], 0.0)
            last.then_inc(zeroed, 1)
            for k in range(2):
                pool.wait_ge(f_mv, k + 1)
                power(RVa[:, :], MVa[:, :, 1], f_eps, k, f_rv)

            def step(n, odd, a, b, c, d):
                u0, u1, u2, u3 = units(n, a, b, c, d)
                add(u1, 1, 2, 1 - odd)
                inverse_deviation(u3)
                add(u1, 1, 3, 1 - odd)
                norm(u2, 1)
                add(u0, 0, 0, odd)
                add(u0, 0, 1, odd)
                norm(u1, 0)
                add(u0, 0, 2, odd)
                add(u0, 0, 3, odd)
                add(u0, 1, 0, odd)
                add(u0, 1, 1, odd)

            def inverse_deviation(q):
                if q is None:
                    return
                pool.wait_ge(mv_done, q + 1)
                power(RV[:, :], MV[:, :, 1], var_eps, q, rv_done)

            def norm(m, t):
                if m is None:
                    return
                pool.wait_ge(p_rsum, 2 * m + t + 1)
                tt(PB[:, t, :, :], PB[:, t, :, :],
                   wide(RS[:, t, :].rearrange("p (h a) -> p h a", a=1), 2, 2 * WIN), ALU.mult).then_inc(p_ready, 1)

            def add(n, t, c, odd):
                if n is None:
                    return
                u, half = 2 * n + t, c % 2
                heads = slice(half * HPC, (half + 1) * HPC)
                cols = slice(half * CH, (half + 1) * CH)
                r = RK[:, heads] if c >= 2 else RQ[:, odd, t, heads]
                pool.wait_ge(sq_summed, 4 * u + c + 1)
                apart(pool)
                ts(r, SSQ[:, t, c // 2, heads], 1e-24, None, ALU.max).then_inc(ss_clamped, 1)
                pool.wait_ge(ss_clamped, 4 * u + c + 1)
                tt(r, r, negh[:, 0:HPC], ALU.pow).then_inc((rq_ready, rk_ready)[c // 2], 1)
                v = T1[:, t, c // 2, cols]
                if c < 2:
                    tt(v, v, T2q[:, t, cols], ALU.add).then_inc(q_ready, 1)
                else:
                    tt(v, v, T2k[:, cols], ALU.add).then_inc(k_added, 1)
                    pool.wait_ge(rk_ready, 2 * u + half + 1)
                    pool.wait_ge(k_added, 2 * u + half + 1)
                    v = v.rearrange("p (k d) -> p k d", k=HPC)
                    tt(v, v, wide(r.rearrange("p (h a) -> p h a", a=1), 2, DH), ALU.mult).then_inc(k_ready, 1)

            pipeline(pool, step, NBL, 3)


_INS = ['x', 'ctx_1024', 'g_xattn', 'g_ffn', 'L0_ffn_Wqkv', 'L0_ffn_q_scale', 'L0_ffn_k_scale', 'L0_ffn_Wo',
        'L0_ffn_ln_g', 'L0_ffn_ln_b', 'L0_ffn_W1', 'L0_ffn_b1', 'L0_ffn_W2', 'L0_ffn_b2']


def constants():
    import numpy as np
    f = np.float32
    half = np.arange(0, DH, 2, dtype=f)
    inv_freq = (f(1.0) / f(10000.0) ** (half / f(DH))).astype(f)
    t = np.arange(SEQ, dtype=f)
    freqs = (t[:, None] * inv_freq[None, :]).astype(f)
    base = ((half + f(0.4 * DH)) / f(1.4 * DH)).astype(f)
    power = ((t - SEQ // 2) / f(WIN // 2)).astype(f)
    scale = (base[None, :] ** power[:, None]).astype(f)
    cos, sin = np.cos(freqs).astype(f), np.sin(freqs).astype(f)
    both = np.stack([scale, f(1.0) / scale], 1)
    cs = (cos[:, None, :] * both).astype(f)
    sn = (sin[:, None, :] * both).astype(f)
    cs = np.concatenate([cs, cs], -1)
    sn = np.concatenate([-sn, sn], -1)
    cs[:, 0] *= f(QK_SCALE)
    sn[:, 0] *= f(QK_SCALE)

    def lay(v):
        return np.ascontiguousarray(v.reshape(TILES, P, -1).transpose(1, 0, 2).reshape(P, -1))

    i, j = np.arange(WIN)[:, None], np.arange(2 * WIN)[None, :]
    seen = (i <= j) & (j <= i + WIN)
    m = np.where(seen, f(0), f(-1e30)).astype(f)
    m = np.tile(m, (SEQ // WIN, 1)).reshape(SEQ // WIN, WIN, 2 * WIN)
    m[0, :, 0:WIN] = -1e30
    return {
        'c_cos': lay(cs), 'c_sin': lay(sn), 'c_mask': lay(m.reshape(SEQ, 2 * WIN)),
        'c_ident': np.eye(P, dtype=f), 'c_shift': np.eye(P, k=1, dtype=f),
        'c_carry': (np.arange(P)[:, None] == P - 1).astype(f) * (np.arange(P)[None, :] == 0).astype(f),
    }


def arrays_of(inputs):
    import numpy as np
    a = {name: np.ascontiguousarray(inputs[name]) for name in _INS}
    for name in ('L0_ffn_ln_g', 'L0_ffn_ln_b'):
        a[name] = np.ascontiguousarray(a[name].T)
    b1 = np.zeros((P, DEPTH, 2, len(FC)), a['L0_ffn_b1'].dtype)
    for half in range(2):
        for c, (f0, fn) in enumerate(FC):
            b1[0:fn, :, half, c] = a['L0_ffn_b1'][:, half * FF + f0:half * FF + f0 + fn].T
    a['L0_ffn_b1'] = b1.reshape(P, -1)
    return a | constants()


def kernel(**inputs):
    import concourse.bacc as bacc
    from concourse.bass_utils import run_bass_kernel_spmd

    nc = bacc.Bacc("TRN2", target_bir_lowering=False, num_devices=1)
    arrays = arrays_of(inputs)
    args = [nc.dram_tensor(f"in_{k}", a.shape, mybir.dt.from_np(a.dtype), kind="ExternalInput").ap()
            for k, a in arrays.items()]
    args.append(nc.dram_tensor("out", (NB, SEQ, D), F32, kind="ExternalOutput").ap())
    flamingo_kernel(nc, *args)
    r = run_bass_kernel_spmd(nc, [{f"in_{k}": a for k, a in arrays.items()}], core_ids=[0])
    return r.results[0]["out"]
```
